# Optimizing a Trainium2 kernel written in Bass

```python
import numpy as np
import jax
import jax.numpy as jnp

def _softmax(x, axis=-1):
    return jax.nn.softmax(x, axis=axis)

def _gelu(x):
    return jax.nn.gelu(x, approximate=True)

def _silu(x):
    return jax.nn.silu(x)

def _sigmoid(x):
    return jax.nn.sigmoid(x)

def _layernorm(x, axis=-1, eps=1e-05):
    m = jnp.mean(x, axis=axis, keepdims=True)
    v = jnp.var(x, axis=axis, keepdims=True)
    return (x - m) / jnp.sqrt(v + eps)

def _scatter_add(tgt, idx, src, axis=0):
    return tgt.at[idx].add(src)

def _segment_sum(src, seg, n):
    return jax.ops.segment_sum(src, seg, n)
kernel_name = 'mk_gnn_resnorm_d2_gnn_r64_f3cad3'

def setup_inputs(seed: int=0):
    np.random.seed(seed)
    _w = jnp.asarray

    def _rec_inputs():
        import jax
        import jax.numpy as jnp
        _gk = jax.random.key(seed)
        x = -0.0003713 + 1 * jax.random.normal(jax.random.fold_in(_gk, 1), (100000, 128), jnp.float32)
        src = jax.random.randint(jax.random.fold_in(_gk, 2), (50000,), 0, 100000, jnp.int32)
        dst = jax.random.randint(jax.random.fold_in(_gk, 3), (50000,), 0, 100000, jnp.int32)
        _o = jnp.argsort(dst, stable=True)
        src = src[_o]
        dst = dst[_o]
        edge_weight = jax.random.uniform(jax.random.fold_in(_gk, 13), (50000,), jnp.float32, 0.0, 0.999999)
        return (x, src, dst, edge_weight)
    x, src, dst, edge_weight = _rec_inputs()

    def _L0_gnn_setup():
        import jax, jax.numpy as jnp
        import numpy as np
        N = 100000
        E = 25000
        D = 128
        EPS = 1e-05

        def gcn_conv(x, W, b, src, dst, w, n):
            h = x @ W
            deg = jax.ops.segment_sum(w, dst, num_segments=n)
            dinv = jnp.where(deg > 0, deg ** (-0.5), 0.0)
            norm = dinv[src] * w * dinv[dst]
            out = jax.ops.segment_sum(h[src] * norm[:, None], dst, num_segments=n)
            return out + b

        def batch_norm(x, gamma, beta):
            m = x.mean(axis=0)
            v = x.var(axis=0)
            return gamma * (x - m) * jax.lax.rsqrt(v + EPS) + beta
        key = jax.random.key(seed)
        ks = jax.random.split(key, 10)
        x = jax.random.normal(ks[0], (N, D), dtype=jnp.float32)
        edge_index = jax.random.randint(ks[1], (2, E), 0, N, dtype=jnp.int64)
        edge_weight = jax.random.uniform(ks[2], (E,), dtype=jnp.float32)
        s = 1.0 / np.sqrt(D)
        W1 = jax.random.uniform(ks[3], (D, D), jnp.float32, -s, s)
        b1 = jax.random.uniform(ks[4], (D,), jnp.float32, -s, s)
        W2 = jax.random.uniform(ks[5], (D, D), jnp.float32, -s, s)
        b2 = jax.random.uniform(ks[6], (D,), jnp.float32, -s, s)
        g1 = jnp.ones((D,), jnp.float32)
        beta1 = jnp.zeros((D,), jnp.float32)
        g2 = jnp.ones((D,), jnp.float32)
        beta2 = jnp.zeros((D,), jnp.float32)
        return {'x': x, 'edge_index': edge_index, 'edge_weight': edge_weight, 'W1': W1, 'b1': b1, 'W2': W2, 'b2': b2, 'g1': g1, 'beta1': beta1, 'g2': g2, 'beta2': beta2}
    _L0_gnn_all = _L0_gnn_setup()
    _L0_gnn_in = {k: v for k, v in _L0_gnn_all.items() if k in ('W1', 'b1', 'W2', 'b2', 'g1', 'beta1', 'g2', 'beta2')}
    del _L0_gnn_all

    def _L1_gnn_setup():
        import jax, jax.numpy as jnp
        import numpy as np
        N_VAR, N_FAC, N_EDGE, D = (100000, 50000, 15625, 128)
        key = jax.random.key(seed)
        ks = jax.random.split(key, 8)
        return {'variables': jax.random.normal(ks[0], (N_VAR, D), dtype=jnp.float32), 'factors': jax.random.normal(ks[1], (N_FAC, D), dtype=jnp.float32), 'senders': jax.random.randint(ks[2], (N_EDGE,), 0, N_VAR), 'receivers': jax.random.randint(ks[3], (N_EDGE,), 0, N_FAC), 'Wm': jax.random.normal(ks[4], (2 * D, D), dtype=jnp.float32) * (1.0 / np.sqrt(2 * D)), 'bm': jnp.zeros((D,), dtype=jnp.float32), 'Wc': jax.random.normal(ks[5], (2 * D, D), dtype=jnp.float32) * (1.0 / np.sqrt(2 * D)), 'bc': jnp.zeros((D,), dtype=jnp.float32)}
    _L1_gnn_all = _L1_gnn_setup()
    _L1_gnn_in = {k: v for k, v in _L1_gnn_all.items() if k in ('factors', 'Wm', 'bm', 'Wc', 'bc')}
    del _L1_gnn_all
    return {'x': x, 'src': src, 'dst': dst, 'edge_weight': edge_weight, 'L0_gnn_W1': _L0_gnn_in['W1'], 'L0_gnn_b1': _L0_gnn_in['b1'], 'L0_gnn_W2': _L0_gnn_in['W2'], 'L0_gnn_b2': _L0_gnn_in['b2'], 'L0_gnn_g1': _L0_gnn_in['g1'], 'L0_gnn_beta1': _L0_gnn_in['beta1'], 'L0_gnn_g2': _L0_gnn_in['g2'], 'L0_gnn_beta2': _L0_gnn_in['beta2'], 'L1_gnn_factors': _L1_gnn_in['factors'], 'L1_gnn_Wm': _L1_gnn_in['Wm'], 'L1_gnn_bm': _L1_gnn_in['bm'], 'L1_gnn_Wc': _L1_gnn_in['Wc'], 'L1_gnn_bc': _L1_gnn_in['bc']}

def reference(x, src, dst, edge_weight, L0_gnn_W1, L0_gnn_b1, L0_gnn_W2, L0_gnn_b2, L0_gnn_g1, L0_gnn_beta1, L0_gnn_g2, L0_gnn_beta2, L1_gnn_factors, L1_gnn_Wm, L1_gnn_bm, L1_gnn_Wc, L1_gnn_bc):
    import jax
    import jax.numpy as jnp

    def _L0_gnn_ref(x, edge_index, edge_weight, W1, b1, W2, b2, g1, beta1, g2, beta2):
        import jax, jax.numpy as jnp
        import numpy as np
        N = 100000
        E = 25000
        D = 128
        EPS = 1e-05

        def gcn_conv(x, W, b, src, dst, w, n):
            h = x @ W
            deg = jax.ops.segment_sum(w, dst, num_segments=n)
            dinv = jnp.where(deg > 0, deg ** (-0.5), 0.0)
            norm = dinv[src] * w * dinv[dst]
            out = jax.ops.segment_sum(h[src] * norm[:, None], dst, num_segments=n)
            return out + b

        def batch_norm(x, gamma, beta):
            m = x.mean(axis=0)
            v = x.var(axis=0)
            return gamma * (x - m) * jax.lax.rsqrt(v + EPS) + beta
        loops = jnp.arange(N, dtype=edge_index.dtype)
        src = jnp.concatenate([edge_index[0], loops])
        dst = jnp.concatenate([edge_index[1], loops])
        w = jnp.concatenate([edge_weight, jnp.ones((N,), edge_weight.dtype)])
        h = gcn_conv(x, W1, b1, src, dst, w, N)
        h = jax.nn.relu(batch_norm(h, g1, beta1))
        h = gcn_conv(h, W2, b2, src, dst, w, N)
        h = jax.nn.relu(batch_norm(h, g2, beta2))
        return h

    def _L1_gnn_ref(variables, factors, senders, receivers, Wm, bm, Wc, bc):
        import jax, jax.numpy as jnp
        import numpy as np
        N_VAR, N_FAC, N_EDGE, D = (100000, 50000, 15625, 128)
        x_i = variables[senders]
        x_j = factors[receivers]
        x = jnp.concatenate([x_i, x_j], axis=-1)
        msg = jax.nn.relu(x @ Wm + bm)
        agg = jax.ops.segment_sum(msg, senders, num_segments=variables.shape[0])
        h = jnp.concatenate([variables, agg], axis=-1)
        h = jax.nn.relu(h @ Wc + bc)
        return variables + h
    edge_index = jnp.stack([src, dst])
    x = _layernorm(x + _L0_gnn_ref(x, edge_index, edge_weight, L0_gnn_W1, L0_gnn_b1, L0_gnn_W2, L0_gnn_b2, L0_gnn_g1, L0_gnn_beta1, L0_gnn_g2, L0_gnn_beta2), axis=-1)
    x = _layernorm(x + _L1_gnn_ref(x, L1_gnn_factors, src, dst, L1_gnn_Wm, L1_gnn_bm, L1_gnn_Wc, L1_gnn_bc), axis=-1)
    return x

_drawn_inputs = setup_inputs


def setup_inputs(seed=0):
    import zlib

    import numpy as np

    out = dict(_drawn_inputs(seed))
    spreads = {'L0_gnn_g1': (1.0, 0.2),
     'L0_gnn_beta1': (0.0, 0.1),
     'L0_gnn_g2': (1.0, 0.2),
     'L0_gnn_beta2': (0.0, 0.1),
     'L1_gnn_bm': (0.0, 0.748),
     'L1_gnn_bc': (0.0, 0.1)}
    factors = {'L0_gnn_b1': 8.0, 'L0_gnn_b2': 8.0}
    for name, (base, spread) in spreads.items():
        noise = np.random.default_rng([zlib.crc32(name.encode()), seed]).standard_normal(out[name].shape)
        drawn = base * np.exp(spread * noise) if base else spread * noise
        out[name] = jnp.asarray(drawn.astype(out[name].dtype))
    for name, factor in factors.items():
        out[name] = (out[name] * factor).astype(out[name].dtype)
    return out
```

```python
from contextlib import ExitStack

import concourse.bass as bass
from concourse import mybir

F32 = mybir.dt.float32
BF16 = mybir.dt.bfloat16
I32 = mybir.dt.int32
ALU = mybir.AluOpType
ACT = mybir.ActivationFunctionType

N = 100000
E = 50000
FACTORS = 50000
D = 128
SLOTS = 4
GROUP = 128 * SLOTS
EPS = 1e-5

NODE_FULL, NODE_TAIL = N // GROUP, (N % GROUP) // SLOTS
EDGE_FULL, EDGE_TAIL = E // GROUP, (E % GROUP) // SLOTS
NODE_GROUPS, EDGE_GROUPS = NODE_FULL + 1, EDGE_FULL + 1
DEG_COLS = NODE_GROUPS * SLOTS
ACC_ROWS = N + GROUP
ZERO_COLS = ACC_ROWS * D // 128 // 48
DMA = 16


def wait(eng, sem, value):
    if not isinstance(value, int) or value > 0:
        eng.wait_ge(sem, value)


def sweep(eng, full, tail, step):
    step(0, 0, 0, 128)
    step(1, 0, 1, 128)
    with eng.Fori(1, full // 2) as turn:
        step(2 * turn, turn, 0, 128)
        step(2 * turn + 1, turn, 1, 128)
    if full % 2:
        step(full - 1, full // 2, 0, 128)
    step(full, full // 2, full % 2, tail)


def wait_apart(eng, C, *waits):
    waits = [(sem, v) for sem, v in waits if not isinstance(v, int) or v > 0]
    for sem, value in waits:
        eng.wait_ge(sem, value)
    if waits:
        eng.sem_inc(C["passed"], 1)


class Chain:

    def __init__(self, eng, sem):
        self.eng, self.sem, self.base, self.n, self.per = eng, sem, 0, 0, None

    def start(self, group):
        self.base, self.n = group * (self.per or 0), 0

    def link(self, ins, apart=None):
        ins.then_inc(self.sem, 1)
        self.n += 1
        if apart is None:
            self.eng.wait_ge(self.sem, self.base + self.n)
        else:
            wait_apart(self.eng, apart, (self.sem, self.base + self.n))

    def end(self):
        self.per = self.per or self.n
        assert self.n == self.per, (self.n, self.per)


def row_groups(x, group, partitions, cols):
    rows = x[bass.ds(group * GROUP, partitions * SLOTS), :]
    return rows.rearrange("(p s) c -> p s c", s=SLOTS)


def item_groups(x, group, partitions):
    return x[bass.ds(group * GROUP, partitions * SLOTS)].rearrange("(p s) -> p s", s=SLOTS)


def build(nc, x, src, dst, w, W1, b1, W2, b2, g1, beta1, g2, beta2, factors, Wm, bm, Wc, bc, out):
    top = ExitStack()
    with top:
        C = {}

        def keep(name, shape, dt=F32):
            C[name] = top.enter_context(nc.sbuf_tensor(name, shape, dt))
            return C[name]

        def dram(name, shape):
            return nc.dram_tensor(name, shape, F32).ap()

        scaled = dram("scaled", (N, D))
        table1 = dram("table1", (N, D + 1))
        table2 = dram("table2", (N, 2 * D))
        sums = [dram(f"sums{i}", (ACC_ROWS, D)) for i in range(3)]

        for name in ("ident", "W1", "W2", "Wm_i", "Wm_j", "Wc_x", "Wc_a"):
            keep(name, [128, 128])
        C["passed"] = top.enter_context(nc.semaphore("passed"))
        keep("one_row", [1, 128])
        keep("bm_row", [1, D])
        keep("bc_row", [1, D])
        keep("vectors", [D, 6])
        keep("earlier", [128, SLOTS, GROUP])
        keep("spare", [128, SLOTS], I32)
        keep("iota_lo", [128, 128])
        keep("iota_col", [128, DEG_COLS])
        keep("zero", [128, ZERO_COLS])
        keep("eps", [128, 1])
        keep("dinv", [128, DEG_COLS])
        keep("bn_rows1", [128, 2, D])
        keep("bn_rows2", [128, 2, D])
        keep("stats", [D, NODE_GROUPS * 6])

        setup(nc, C, W1, W2, Wm, Wc, bm, bc, (b1, g1, beta1, b2, g2, beta2))
        degrees(nc, C, dst, w, sums)
        scale_nodes(nc, C, x, scaled)
        edges(nc, C, "e1", 1, src, dst, w, scaled, sums[0], factors)
        nodes(nc, C, "n1", 1, x, scaled, sums[0], table1)
        norm_rows(nc, C, "m1", 0, C["bn_rows1"])
        edges(nc, C, "e2", 2, src, dst, w, table1, sums[1], factors)
        nodes(nc, C, "n2", 2, x, table1, sums[1], table2)
        norm_rows(nc, C, "m2", 3, C["bn_rows2"])
        edges(nc, C, "e3", 3, src, dst, w, table2, sums[2], factors)
        nodes(nc, C, "n3", 3, x, table2, sums[2], out)


def setup(nc, C, W1, W2, Wm, Wc, bm, bc, vectors):
    with ExitStack() as ctx:
        loaded = ctx.enter_context(nc.semaphore("setup_loaded"))
        filled = ctx.enter_context(nc.semaphore("setup_filled"))
        block = ctx.enter_context(nc.Block())

        @block.sync
        def _(sp):
            n = 0
            for name, part in (("W1", W1), ("W2", W2), ("Wm_i", Wm[0:D, :]), ("Wm_j", Wm[D:2 * D, :]),
                               ("Wc_x", Wc[0:D, :]), ("Wc_a", Wc[D:2 * D, :])):
                sp.dma_start(C[name][:, :], part).then_inc(loaded, DMA)
                n += 1
            for name, row in (("bm_row", bm), ("bc_row", bc)):
                sp.dma_start(C[name][:, :], row.rearrange("(o n) -> o n", o=1)).then_inc(loaded, DMA)
                n += 1
            for i, v in enumerate(vectors):
                sp.dma_start(C["vectors"][:, i:i + 1], v.rearrange("(n o) -> n o", o=1)).then_inc(loaded, DMA)
                n += 1
            sp.wait_ge(loaded, DMA * n)

        @block.gpsimd
        def _(pool):
            pool.memset(C["ident"][:, :], 0.0).then_inc(filled, 1)
            pool.memset(C["earlier"][:, :, :], 1.0).then_inc(filled, 1)
            pool.iota(C["spare"][:, :], pattern=[[1, SLOTS]], base=N, channel_multiplier=SLOTS)
            pool.iota(C["iota_lo"][:, :], pattern=[[1, 128]], base=0, channel_multiplier=0,
                      allow_small_or_imprecise_dtypes=True)
            pool.iota(C["iota_col"][:, :], pattern=[[1, DEG_COLS]], base=0, channel_multiplier=0,
                      allow_small_or_imprecise_dtypes=True)
            pool.wait_ge(filled, 2)
            pool.affine_select(out=C["ident"][:, :], in_=C["ident"][:, :], compare_op=ALU.not_equal, fill=1.0,
                               base=0, pattern=[[-1, 128]], channel_multiplier=1)
            for s in range(SLOTS):
                pool.affine_select(out=C["earlier"][:, s, :], in_=C["earlier"][:, s, :], compare_op=ALU.is_gt,
                                   fill=0.0, base=s, pattern=[[-1, GROUP]], channel_multiplier=SLOTS)

        @block.vector
        def _(dve):
            nc.vector.memset(C["one_row"][:, :], 1.0)
            nc.vector.memset(C["zero"][:, :], 0.0)
            nc.vector.memset(C["eps"][:, :], EPS)


def degrees(nc, C, dst, w, sums):
    HALF = DEG_COLS // 2
    with ExitStack() as ctx:
        sb = lambda name, shape, dt=F32: ctx.enter_context(nc.sbuf_tensor("d_" + name, shape, dt))
        sem = lambda name: ctx.enter_context(nc.semaphore("d_" + name))
        ids = [sb(f"ids{q}", [128, SLOTS], I32) for q in range(2)]
        ws = [sb(f"ws{q}", [128, SLOTS]) for q in range(2)]
        lo_i = sb("lo_i", [128, SLOTS], I32)
        hi_i = sb("hi_i", [128, SLOTS], I32)
        low2 = sb("low2", [128, SLOTS], I32)
        col_i = sb("col_i", [128, SLOTS], I32)
        lo = sb("lo", [128, SLOTS])
        col = sb("col", [128, SLOTS])
        part_b = sb("part_b", [128, SLOTS], BF16)
        parts = sb("parts", [128, 3, SLOTS])
        rest = sb("rest", [128, SLOTS])
        hot_lo = [sb(f"hot_lo{q}", [128, SLOTS, 3, 128], BF16) for q in range(2)]
        hot_col = [sb(f"hot_col{q}", [128, SLOTS, DEG_COLS], BF16) for q in range(2)]
        zero_b = sb("zero_b", [128, 512], BF16)
        positive = sb("positive", [128, DEG_COLS])
        root = sb("root", [128, DEG_COLS])
        deg = [ctx.enter_context(nc.psum_tensor(f"d_deg{i}", [128, 512], F32)) for i in range(2)]
        loaded = [sem(f"loaded{q}") for q in range(2)]
        chain_sem, hot_ready, hot_used = sem("chain"), sem("hot_ready"), sem("hot_used")
        zero_ready, zeroed, rooted, clamped = sem("zero_ready"), sem("zeroed"), sem("rooted"), sem("clamped")
        block = ctx.enter_context(nc.Block())

        @block.sync
        def _(sp):
            def step(g, turn, q, P):
                wait(sp, hot_ready, g - 1)
                sp.dma_start(ids[q][0:P, :], item_groups(dst, g, P)).then_inc(loaded[q], DMA)
                sp.dma_start(ws[q][0:P, :], item_groups(w, g, P)).then_inc(loaded[q], DMA)
            sweep(sp, EDGE_FULL, EDGE_TAIL, step)

        @block.scalar
        def _(act):
            for s in sums:
                flat = s.rearrange("r c -> (r c)").rearrange("(p k c) -> p k c", p=128, c=ZERO_COLS)
                for k in range(48):
                    act.dma_start(flat[:, k, :], C["zero"][:, :]).then_inc(zeroed, DMA)
            act.wait_ge(clamped, 1)
            nc.scalar.activation(root[:, :], C["dinv"][:, :], ACT.Sqrt).then_inc(rooted, 1)
            act.wait_ge(zeroed, DMA * 48 * 3)

        @block.vector
        def _(dve):
            ch = Chain(dve, chain_sem)
            nc.vector.memset(zero_b[:, :], 0.0).then_inc(zero_ready, 1)

            def step(g, turn, q, P):
                ch.start(g)
                wait(dve, hot_ready, g)
                dve.wait_ge(loaded[q], 2 * DMA * turn + 2 * DMA)
                nc.vector.tensor_scalar(lo_i[0:P, :], ids[q][0:P, :], 2, 127, ALU.logical_shift_right, ALU.bitwise_and)
                nc.vector.tensor_scalar(hi_i[0:P, :], ids[q][0:P, :], 9, 2, ALU.logical_shift_right, ALU.logical_shift_left)
                nc.vector.tensor_scalar(low2[0:P, :], ids[q][0:P, :], 3, None, ALU.bitwise_and)
                ch.link(nc.vector.tensor_copy(part_b[0:P, :], ws[q][0:P, :]))
                nc.vector.tensor_copy(parts[0:P, 0, :], part_b[0:P, :])
                ch.link(nc.vector.tensor_tensor(col_i[0:P, :], hi_i[0:P, :], low2[0:P, :], ALU.bitwise_or))
                nc.vector.tensor_copy(lo[0:P, :], lo_i[0:P, :])
                nc.vector.tensor_copy(col[0:P, :], col_i[0:P, :])
                ch.link(nc.vector.tensor_tensor(rest[0:P, :], ws[q][0:P, :], parts[0:P, 0, :], ALU.subtract))
                ch.link(nc.vector.tensor_copy(part_b[0:P, :], rest[0:P, :]))
                ch.link(nc.vector.tensor_copy(parts[0:P, 1, :], part_b[0:P, :]))
                ch.link(nc.vector.tensor_tensor(parts[0:P, 2, :], rest[0:P, :], parts[0:P, 1, :], ALU.subtract))
                wait(dve, hot_used, g - 1)
                for s in range(SLOTS):
                    nc.vector.tensor_scalar(hot_col[q][0:P, s, :], C["iota_col"][0:P, :], col[0:P, s:s + 1], None,
                                            ALU.is_equal)
                    for k in range(3):
                        last = nc.vector.tensor_scalar(hot_lo[q][0:P, s, k, :], C["iota_lo"][0:P, :], lo[0:P, s:s + 1],
                                                       parts[0:P, k, s:s + 1], ALU.is_equal, ALU.mult)
                last.then_inc(hot_ready, 1)
                ch.end()
            sweep(dve, EDGE_FULL, EDGE_TAIL, step)
            dve.wait_ge(hot_used, EDGE_GROUPS + 1)
            ch.start(EDGE_GROUPS)
            nc.vector.tensor_scalar(C["dinv"][:, 0:HALF], deg[0][:, 0:HALF], 1.0, None, ALU.add)
            ch.link(nc.vector.tensor_scalar(C["dinv"][:, HALF:], deg[1][:, 0:HALF], 1.0, None, ALU.add))
            ch.link(nc.vector.tensor_scalar(positive[:, :], C["dinv"][:, :], 0.0, None, ALU.is_gt))
            ch.link(nc.vector.scalar_tensor_tensor(C["dinv"][:, :], C["dinv"][:, :], 1.0, positive[:, :],
                                                   ALU.subtract, ALU.mult))
            ch.link(nc.vector.tensor_scalar(C["dinv"][:, :], C["dinv"][:, :], 1.0, None, ALU.add))
            nc.vector.memset(root[:, 0:1], 0.0).then_inc(clamped, 1)
            dve.wait_ge(rooted, 1)
            ch.link(nc.vector.reciprocal(root[:, :], root[:, :]))
            ch.link(nc.vector.tensor_tensor(C["dinv"][:, :], root[:, :], positive[:, :], ALU.mult))

        @block.tensor
        def _(pe):
            pe.wait_ge(zero_ready, 1)
            for i in range(2):
                nc.tensor.matmul(deg[i][:, 0:HALF], zero_b[:, 0:128], zero_b[:, 0:HALF], start=True, stop=False)

            def step(g, turn, q, P):
                pe.wait_ge(hot_ready, g + 1)
                for s in range(SLOTS):
                    for k in range(3):
                        for i in range(2):
                            last = nc.tensor.matmul(deg[i][:, 0:HALF], hot_lo[q][0:P, s, k, :],
                                                    hot_col[q][0:P, s, i * HALF:(i + 1) * HALF], start=False,
                                                    stop=False)
                last.then_inc(hot_used, 1)
            sweep(pe, EDGE_FULL, EDGE_TAIL, step)
            for i in range(2):
                last = nc.tensor.matmul(deg[i][:, 0:HALF], zero_b[:, 0:128], zero_b[:, 0:HALF], start=False, stop=True)
            last.then_inc(hot_used, 1)


def scale_nodes(nc, C, x, scaled):
    with ExitStack() as ctx:
        xin = [ctx.enter_context(nc.sbuf_tensor(f"s_in{q}", [128, SLOTS, D], F32)) for q in range(2)]
        xout = [ctx.enter_context(nc.sbuf_tensor(f"s_out{q}", [128, SLOTS, D], F32)) for q in range(2)]
        loaded = [ctx.enter_context(nc.semaphore(f"s_loaded{q}")) for q in range(2)]
        stored = [ctx.enter_context(nc.semaphore(f"s_stored{q}")) for q in range(2)]
        done = ctx.enter_context(nc.semaphore("s_done"))
        block = ctx.enter_context(nc.Block())

        @block.sync
        def _(sp):
            def step(g, turn, q, P):
                wait(sp, done, g - 1)
                sp.dma_start(xin[q][0:P], row_groups(x, g, P, D)).then_inc(loaded[q], DMA)
            sweep(sp, NODE_FULL, NODE_TAIL, step)

        @block.scalar
        def _(act):
            def step(g, turn, q, P):
                act.wait_ge(done, g + 1)
                act.dma_start(row_groups(scaled, g, P, D), xout[q][0:P]).then_inc(stored[q], DMA)
            sweep(act, NODE_FULL, NODE_TAIL, step)
            for q in range(2):
                act.wait_ge(stored[q], DMA * (NODE_GROUPS // 2))

        @block.vector
        def _(dve):
            def step(g, turn, q, P):
                dve.wait_ge(loaded[q], DMA * turn + DMA)
                wait(dve, stored[q], DMA * turn)
                d = C["dinv"][0:P, bass.ds(g * SLOTS, SLOTS)].unsqueeze(2).to_broadcast([P, SLOTS, D])
                nc.vector.tensor_tensor(xout[q][0:P], xin[q][0:P], d, ALU.mult).then_inc(done, 1)
            sweep(dve, NODE_FULL, NODE_TAIL, step)


def edges(nc, C, ph, kind, src, dst, w, table, sums, factors):
    cols = {1: D, 2: D + 1, 3: 2 * D}[kind]
    key_of = src if kind == 3 else dst
    LOADS = 5 if kind == 3 else 4
    with ExitStack() as ctx:
        sb = lambda name, shape, dt=F32: [ctx.enter_context(nc.sbuf_tensor(f"{ph}_{name}{q}", shape, dt)) for q in range(2)]
        one = lambda name, shape, dt=F32: ctx.enter_context(nc.sbuf_tensor(f"{ph}_{name}", shape, dt))
        ps = lambda name: [ctx.enter_context(nc.psum_tensor(f"{ph}_{name}{q}", [128, GROUP], F32)) for q in range(2)]
        sem = lambda name: ctx.enter_context(nc.semaphore(f"{ph}_{name}"))
        from_id = sb("from", [128, SLOTS], I32)
        key = sb("key", [128, SLOTS], I32)
        keys = sb("keys", [128, GROUP], I32)
        wt = sb("w", [128, SLOTS])
        rows = sb("rows", [128, SLOTS, cols])
        equal = sb("equal", [128, SLOTS, GROUP])
        add_at = sb("add_at", [128, SLOTS], I32)
        summed = sb("summed", [128, SLOTS, D])
        key_f = one("key_f", [128, SLOTS])
        junk = one("junk", [128, SLOTS, GROUP], BF16)
        before = one("before", [128, SLOTS])
        away = one("away", [128, SLOTS])
        coef = one("coef", [128, SLOTS])
        ps_sum = ps("ps_sum")
        loaded = [sem(f"loaded{q}") for q in range(2)]
        gathered = [sem(f"gathered{q}") for q in range(2)]
        dve_chain, equal_ready = sem("dve_chain"), sem("equal_ready")
        combined, sum_ready, scattered, added_at = sem("combined"), sem("sum_ready"), sem("scattered"), sem("added_at")
        if kind >= 2:
            msg = sb("msg", [128, SLOTS, D])
            normed, msg_ready = sem("normed"), sem("msg_ready")
        if kind == 3:
            fac_id = sb("fac_id", [128, SLOTS], I32)
            dsts = sb("dsts", [128, SLOTS], I32)
            fac = sb("fac", [128, SLOTS, D])
            y = one("y", [128, SLOTS, D])
            st = one("st", [128, SLOTS, 6])
            mv = one("mv", [128, SLOTS, 2])
            sd = one("sd", [128, SLOTS])
            rstd = one("rstd", [128, SLOTS])
            v = sb("v", [128, SLOTS, D])
            vT = sb("vT", [128, GROUP])
            fT = sb("fT", [128, GROUP])
            ps_vT, ps_fT, ps_msg = ps("ps_vT"), ps("ps_fT"), ps("ps_msg")
            fac_ready, var_ready, sd_ready, v_ready = sem("fac_ready"), sem("var_ready"), sem("sd_ready"), sem("v_ready")
            turned, turned_out, mixed = sem("turned"), sem("turned_out"), sem("mixed")
        block = ctx.enter_context(nc.Block())

        @block.sync
        def _(sp):
            def step(g, turn, q, P):
                wait(sp, equal_ready, g - 1)
                W = P * SLOTS
                sp.dma_start(from_id[q][0:P, :], item_groups(src, g, P)).then_inc(loaded[q], DMA)
                sp.dma_start(key[q][0:P, :], item_groups(key_of, g, P)).then_inc(loaded[q], DMA)
                sp.dma_start(wt[q][0:P, :], item_groups(w, g, P)).then_inc(loaded[q], DMA)
                sp.dma_start(keys[q][0:P, 0:W], key_of[bass.ds(g * GROUP, W)].partition_broadcast(P))\
                    .then_inc(loaded[q], DMA)
                if kind == 3:
                    sp.dma_start(dsts[q][0:P, :], item_groups(dst, g, P)).then_inc(loaded[q], DMA)
            sweep(sp, EDGE_FULL, EDGE_TAIL, step)

        @block.gpsimd
        def _(pool):

            def scatter(g, q, P):
                wait_apart(pool, C, (sum_ready, g + 1), (added_at, g + 1), (scattered, DMA * SLOTS * g))
                for s in range(SLOTS):
                    pool.indirect_dma_start(out=sums, out_offset=bass.IndirectOffsetOnAxis(ap=add_at[q][0:P, s:s + 1], axis=0),
                                            in_=summed[q][0:P, s, :], in_offset=None, compute_op=ALU.add)\
                        .then_inc(scattered, DMA)

            def step(g, turn, q, P):
                wait_apart(pool, C, (loaded[q], LOADS * DMA * turn + LOADS * DMA),
                           (combined if kind == 1 else normed, g - 1))
                for s in range(SLOTS):
                    pool.indirect_dma_start(out=rows[q][0:P, s, :], out_offset=None, in_=table,
                                            in_offset=bass.IndirectOffsetOnAxis(ap=from_id[q][0:P, s:s + 1], axis=0))\
                        .then_inc(gathered[q], DMA)
                if kind == 3:
                    wait_apart(pool, C, (fac_ready, g + 1), (turned, g - 1))
                    for s in range(SLOTS):
                        pool.indirect_dma_start(out=fac[q][0:P, s, :], out_offset=None, in_=factors,
                                                in_offset=bass.IndirectOffsetOnAxis(ap=fac_id[q][0:P, s:s + 1], axis=0))\
                            .then_inc(gathered[q], DMA)
                if not isinstance(g, int) or g > 0:
                    scatter(g - 1, 1 - q, 128)
            sweep(pool, EDGE_FULL, EDGE_TAIL, step)
            scatter(EDGE_FULL, EDGE_FULL % 2, EDGE_TAIL)
            pool.wait_ge(scattered, DMA * SLOTS * EDGE_GROUPS)

        gathers = SLOTS * (2 if kind == 3 else 1)

        @block.vector
        def _(dve):
            ch = Chain(dve, dve_chain)
            bn = C["bn_rows2"] if kind == 3 else C["bn_rows1"]

            def step(g, turn, q, P):
                W = P * SLOTS
                ch.start(g)
                wait(dve, equal_ready if kind == 1 else normed if kind == 2 else v_ready, g)
                dve.wait_ge(loaded[q], LOADS * DMA * turn + LOADS * DMA)
                if kind == 3:
                    wait(dve, turned, g - 1)
                    nc.vector.tensor_scalar(fac_id[q][0:P, :], dsts[q][0:P, :], float(FACTORS - 1), None,
                                            ALU.min).then_inc(fac_ready, 1)
                nc.vector.tensor_copy(key_f[0:P, :], key[q][0:P, :])
                ch.link(nc.vector.tensor_tensor(away[0:P, :], C["spare"][0:P, :], key[q][0:P, :], ALU.subtract))
                for s in range(SLOTS):
                    last = nc.vector.scalar_tensor_tensor(junk[0:P, s, 0:W], keys[q][0:P, 0:W], key_f[0:P, s:s + 1],
                                                          C["earlier"][0:P, s, 0:W], ALU.is_equal, ALU.mult,
                                                          accum_out=before[0:P, s:s + 1])
                ch.link(last)
                ch.link(nc.vector.scalar_tensor_tensor(away[0:P, :], before[0:P, :], 0.0, away[0:P, :], ALU.is_gt, ALU.mult))
                wait(dve, scattered, DMA * SLOTS * (g - 1))
                nc.vector.tensor_tensor(add_at[q][0:P, :], away[0:P, :], key[q][0:P, :], ALU.add).then_inc(added_at, 1)
                dve.wait_ge(gathered[q], gathers * DMA * turn + gathers * DMA)
                if kind == 2:
                    ch.link(nc.vector.tensor_tensor(coef[0:P, :], wt[q][0:P, :], rows[q][0:P, :, D], ALU.mult))
                wait(dve, combined, g - 1)
                for s in range(SLOTS):
                    c = {1: wt[q], 2: coef, 3: None}[kind]
                    if c is None:
                        last = nc.vector.tensor_scalar(equal[q][0:P, s, 0:W], keys[q][0:P, 0:W], key_f[0:P, s:s + 1],
                                                       None, ALU.is_equal)
                    else:
                        last = nc.vector.tensor_scalar(equal[q][0:P, s, 0:W], keys[q][0:P, 0:W], key_f[0:P, s:s + 1],
                                                       c[0:P, s:s + 1], ALU.is_equal, ALU.mult)
                last.then_inc(equal_ready, 1)
                if kind == 2:
                    scale = bn[0:P, 0:1, :].to_broadcast([P, SLOTS, D])
                    shift = bn[0:P, 1:2, :].to_broadcast([P, SLOTS, D])
                    ch.link(nc.vector.tensor_tensor(msg[q][0:P], rows[q][0:P, :, 0:D], scale, ALU.mult))
                    ch.link(nc.vector.tensor_tensor(msg[q][0:P], msg[q][0:P], shift, ALU.add))
                    nc.vector.tensor_scalar(msg[q][0:P], msg[q][0:P], 0.0, None, ALU.max).then_inc(normed, 1)
                if kind == 3:
                    scale = bn[0:P, 0:1, :].to_broadcast([P, SLOTS, D])
                    shift = bn[0:P, 1:2, :].to_broadcast([P, SLOTS, D])
                    ch.link(nc.vector.tensor_tensor(y[0:P], rows[q][0:P, :, 0:D], scale, ALU.mult))
                    ch.link(nc.vector.tensor_tensor(y[0:P], y[0:P], shift, ALU.add))
                    nc.vector.scalar_tensor_tensor(y[0:P], y[0:P], 0.0, rows[q][0:P, :, D:2 * D], ALU.max, ALU.add)\
                        .then_inc(normed, 1)
                    dve.wait_ge(normed, g + 1)
                    for s in range(SLOTS):
                        last = nc.vector.bn_stats(st[0:P, s, :], y[0:P, s, :])
                    ch.link(last, apart=C)
                    for s in range(SLOTS):
                        last = nc.vector.bn_aggr(mv[0:P, s, :], st[0:P, s, :])
                    last.then_inc(var_ready, 1)
                    dve.wait_ge(sd_ready, g + 1)
                    ch.link(nc.vector.reciprocal(rstd[0:P, :], sd[0:P, :]))
                    wait(dve, turned, g - 1)
                    for s in range(SLOTS):
                        last = nc.vector.tensor_scalar(v[q][0:P, s, :], y[0:P, s, :], mv[0:P, s, 0:1],
                                                       rstd[0:P, s:s + 1], ALU.subtract, ALU.mult)
                    last.then_inc(v_ready, 1)
                ch.end()
            sweep(dve, EDGE_FULL, EDGE_TAIL, step)

        @block.tensor
        def _(pe):
            def step(g, turn, q, P):
                if kind == 3:
                    pe.wait_ge(v_ready, g + 1)
                    pe.wait_ge(gathered[q], gathers * DMA * turn + gathers * DMA)
                    wait(pe, turned_out, 2 * (g - 1))
                    for s in range(SLOTS):
                        nc.tensor.transpose(ps_vT[q][:, s * P:(s + 1) * P], v[q][0:P, s, :], C["ident"][0:P, 0:P])
                    for s in range(SLOTS):
                        last = nc.tensor.transpose(ps_fT[q][:, s * P:(s + 1) * P], fac[q][0:P, s, :],
                                                   C["ident"][0:P, 0:P])
                    last.then_inc(turned, 1)
                    pe.wait_ge(turned_out, 2 * g + 2)
                    wait(pe, msg_ready, g - 1)
                    for s in range(SLOTS):
                        o = ps_msg[q][0:P, s * D:(s + 1) * D]
                        nc.tensor.matmul(o, vT[q][:, s * P:(s + 1) * P], C["Wm_i"][:, :], start=True, stop=False)
                        nc.tensor.matmul(o, fT[q][:, s * P:(s + 1) * P], C["Wm_j"][:, :], start=False, stop=False)
                        last = nc.tensor.matmul(o, C["one_row"][:, 0:P], C["bm_row"][:, :], start=False, stop=True)
                    last.then_inc(mixed, 1)
                if kind == 1:
                    pe.wait_ge(gathered[q], gathers * DMA * turn + gathers * DMA)
                    m_rows = rows[q]
                elif kind == 2:
                    pe.wait_ge(normed, g + 1)
                    m_rows = msg[q]
                else:
                    pe.wait_ge(msg_ready, g + 1)
                    m_rows = msg[q]
                pe.wait_ge(equal_ready, g + 1)
                wait(pe, sum_ready, g - 1)
                for m in range(SLOTS):
                    for s in range(SLOTS):
                        last = nc.tensor.matmul(ps_sum[q][0:P, m * D:(m + 1) * D],
                                                equal[q][0:P, s, m:P * SLOTS:SLOTS], m_rows[0:P, s, 0:D],
                                                start=(s == 0), stop=(s == SLOTS - 1))
                last.then_inc(combined, 1)
            sweep(pe, EDGE_FULL, EDGE_TAIL, step)

        @block.scalar
        def _(act):
            def step(g, turn, q, P):
                W = P * SLOTS
                if kind == 3:
                    act.wait_ge(var_ready, g + 1)
                    nc.scalar.activation(sd[0:P, :], mv[0:P, :, 1], ACT.Sqrt, bias=C["eps"][0:P, :]).then_inc(sd_ready, 1)
                    act.wait_ge(turned, g + 1)
                    wait(act, mixed, g - 1)
                    nc.scalar.copy(vT[q][:, 0:W], ps_vT[q][:, 0:W]).then_inc(turned_out, 1)
                    nc.scalar.copy(fT[q][:, 0:W], ps_fT[q][:, 0:W]).then_inc(turned_out, 1)
                    act.wait_ge(mixed, g + 1)
                    wait(act, combined, g - 1)
                    nc.scalar.activation(msg[q][0:P].rearrange("p s c -> p (s c)"), ps_msg[q][0:P, :], ACT.Relu)\
                        .then_inc(msg_ready, 1)
                act.wait_ge(combined, g + 1)
                wait(act, scattered, DMA * SLOTS * (g - 1))
                nc.scalar.copy(summed[q][0:P].rearrange("p s c -> p (s c)"), ps_sum[q][0:P, :]).then_inc(sum_ready, 1)
            sweep(act, EDGE_FULL, EDGE_TAIL, step)


def nodes(nc, C, ph, kind, x, table, sums, out):
    in_cols = {1: D, 2: D + 1, 3: 2 * D}[kind]
    out_cols = {1: D + 1, 2: 2 * D, 3: D}[kind]
    LOADS = 2 if kind != 2 else 3
    Wt = {1: "W1", 2: "W2"}.get(kind)
    with ExitStack() as ctx:
        sb = lambda name, shape, dt=F32: [ctx.enter_context(nc.sbuf_tensor(f"{ph}_{name}{q}", shape, dt)) for q in range(2)]
        one = lambda name, shape, dt=F32: ctx.enter_context(nc.sbuf_tensor(f"{ph}_{name}", shape, dt))
        ps = lambda name: [ctx.enter_context(nc.psum_tensor(f"{ph}_{name}{q}", [128, GROUP], F32)) for q in range(2)]
        sem = lambda name: ctx.enter_context(nc.semaphore(f"{ph}_{name}"))
        rows = sb("rows", [128, SLOTS, in_cols])
        sin = sb("sin", [128, SLOTS, D])
        res = sb("res", [128, SLOTS, out_cols])
        z = sb("z", [128, SLOTS, D])
        zT = sb("zT", [128, GROUP])
        ps_zT, ps_out = ps("ps_zT"), ps("ps_out")
        loaded = [sem(f"loaded{q}") for q in range(2)]
        stored = [sem(f"stored{q}") for q in range(2)]
        chain_sem, z_ready, turned, turned_out = sem("chain"), sem("z_ready"), sem("turned"), sem("turned_out")
        mixed, res_ready, stats_done = sem("mixed"), sem("res_ready"), sem("stats_done")
        if kind != 3:
            ps_flat = ps("ps_flat")
            dinv_ready = sem("dinv_ready")
        else:
            y = sb("y", [128, SLOTS, D])
            h = sb("h", [128, SLOTS, D])
            h_ready = sem("h_ready")
            st = one("st", [128, SLOTS, 6])
            mv = one("mv", [128, SLOTS, 2])
            sd = one("sd", [128, SLOTS])
            rstd = one("rstd", [128, SLOTS])
            mv2 = one("mv2", [128, SLOTS, 2])
            sd2 = one("sd2", [128, SLOTS])
            rstd2 = one("rstd2", [128, SLOTS])
            sT = sb("sT", [128, GROUP])
            ps_sT = ps("ps_sT")
            var_ready, sd_ready = sem("var_ready"), sem("sd_ready")
            var2_ready, sd2_ready, y_ready = sem("var2_ready"), sem("sd2_ready"), sem("y_ready")
        block = ctx.enter_context(nc.Block())

        @block.sync
        def _(sp):
            def step(g, turn, q, P):
                wait(sp, res_ready, g - 1)
                sp.dma_start(rows[q][0:P], row_groups(table, g, P, in_cols)).then_inc(loaded[q], DMA)
                sp.dma_start(sin[q][0:P], row_groups(sums, g, P, D)).then_inc(loaded[q], DMA)
                if kind == 2:
                    wait(sp, stored[q], DMA * turn)
                    sp.dma_start(res[q][0:P, :, D:2 * D], row_groups(x, g, P, D)).then_inc(loaded[q], DMA)
            sweep(sp, NODE_FULL, NODE_TAIL, step)

        @block.gpsimd
        def _(pool):
            def step(g, turn, q, P):
                pool.wait_ge(res_ready, g + 1)
                if kind == 2:
                    pool.wait_ge(loaded[q], LOADS * DMA * turn + LOADS * DMA)
                pool.dma_start(row_groups(out, g, P, out_cols), res[q][0:P]).then_inc(stored[q], DMA)
            sweep(pool, NODE_FULL, NODE_TAIL, step)
            for q in range(2):
                pool.wait_ge(stored[q], DMA * (NODE_GROUPS // 2))

        @block.vector
        def _(dve):
            ch = Chain(dve, chain_sem)
            bn = C["bn_rows2"] if kind == 3 else C["bn_rows1"]

            def step(g, turn, q, P):
                W = P * SLOTS
                ch.start(g)
                wait(dve, stats_done if kind != 3 else res_ready, g)
                dve.wait_ge(loaded[q], LOADS * DMA * turn + LOADS * DMA)
                scale = bn[0:P, 0:1, :].to_broadcast([P, SLOTS, D])
                shift = bn[0:P, 1:2, :].to_broadcast([P, SLOTS, D])
                dinv = C["dinv"][0:P, bass.ds(g * SLOTS, SLOTS)].unsqueeze(2).to_broadcast([P, SLOTS, D])
                if kind == 1:
                    wait(dve, turned, g - 1)
                    ch.link(nc.vector.tensor_tensor(z[q][0:P], rows[q][0:P], sin[q][0:P], ALU.add))
                    nc.vector.tensor_tensor(z[q][0:P], z[q][0:P], dinv, ALU.mult).then_inc(z_ready, 1)
                elif kind == 2:
                    wait(dve, turned, g - 1)
                    ch.link(nc.vector.tensor_tensor(z[q][0:P], rows[q][0:P, :, 0:D], scale, ALU.mult))
                    ch.link(nc.vector.tensor_tensor(z[q][0:P], z[q][0:P], shift, ALU.add))
                    ch.link(nc.vector.scalar_tensor_tensor(z[q][0:P], z[q][0:P], 0.0, dinv, ALU.max, ALU.mult))
                    ch.link(nc.vector.tensor_tensor(z[q][0:P], z[q][0:P], sin[q][0:P], ALU.add))
                    nc.vector.tensor_tensor(z[q][0:P], z[q][0:P], dinv, ALU.mult).then_inc(z_ready, 1)
                else:
                    ch.link(nc.vector.tensor_tensor(y[q][0:P], rows[q][0:P, :, 0:D], scale, ALU.mult))
                    ch.link(nc.vector.tensor_tensor(y[q][0:P], y[q][0:P], shift, ALU.add))
                    ch.link(nc.vector.scalar_tensor_tensor(y[q][0:P], y[q][0:P], 0.0, rows[q][0:P, :, D:2 * D],
                                                           ALU.max, ALU.add))
                    for s in range(SLOTS):
                        last = nc.vector.bn_stats(st[0:P, s, :], y[q][0:P, s, :])
                    ch.link(last, apart=C)
                    for s in range(SLOTS):
                        last = nc.vector.bn_aggr(mv[0:P, s, :], st[0:P, s, :])
                    last.then_inc(var_ready, 1)
                    dve.wait_ge(sd_ready, g + 1)
                    ch.link(nc.vector.reciprocal(rstd[0:P, :], sd[0:P, :]))
                    wait(dve, turned, g - 1)
                    for s in range(SLOTS):
                        last = nc.vector.tensor_scalar(z[q][0:P, s, :], y[q][0:P, s, :], mv[0:P, s, 0:1],
                                                       rstd[0:P, s:s + 1], ALU.subtract, ALU.mult)
                    last.then_inc(z_ready, 1)
                if kind != 3:
                    dve.wait_ge(mixed, g + 1)
                    nc.vector.bn_stats(C["stats"][:, bass.ds(g * 6, 6)], ps_flat[q][:, 0:W]).then_inc(stats_done, 1)
                    if kind == 1:
                        wait_apart(dve, C, (stored[q], DMA * turn))
                        nc.vector.tensor_copy(res[q][0:P, :, D], C["dinv"][0:P, bass.ds(g * SLOTS, SLOTS)])\
                            .then_inc(dinv_ready, 1)
                else:
                    dve.wait_ge(h_ready, g + 1)
                    dve.wait_ge(z_ready, g + 1)
                    ch.link(nc.vector.scalar_tensor_tensor(y[q][0:P], z[q][0:P], 2.0, h[q][0:P], ALU.mult, ALU.add))
                    for s in range(SLOTS):
                        last = nc.vector.bn_stats(st[0:P, s, :], y[q][0:P, s, :])
                    ch.link(last, apart=C)
                    for s in range(SLOTS):
                        last = nc.vector.bn_aggr(mv2[0:P, s, :], st[0:P, s, :])
                    last.then_inc(var2_ready, 1)
                    dve.wait_ge(sd2_ready, g + 1)
                    ch.link(nc.vector.reciprocal(rstd2[0:P, :], sd2[0:P, :]))
                    wait(dve, stored[q], DMA * turn)
                    for s in range(SLOTS):
                        last = nc.vector.tensor_scalar(res[q][0:P, s, :], y[q][0:P, s, :], mv2[0:P, s, 0:1],
                                                       rstd2[0:P, s:s + 1], ALU.subtract, ALU.mult)
                    last.then_inc(res_ready, 1)
                ch.end()
            sweep(dve, NODE_FULL, NODE_TAIL, step)

        @block.tensor
        def _(pe):
            def step(g, turn, q, P):
                W = P * SLOTS
                pe.wait_ge(z_ready, g + 1)
                wait(pe, turned_out, (2 if kind == 3 else 1) * (g - 1))
                for s in range(SLOTS):
                    last = nc.tensor.transpose(ps_zT[q][:, s * P:(s + 1) * P], z[q][0:P, s, :], C["ident"][0:P, 0:P])
                if kind == 3:
                    pe.wait_ge(loaded[q], LOADS * DMA * turn + LOADS * DMA)
                    for s in range(SLOTS):
                        last = nc.tensor.transpose(ps_sT[q][:, s * P:(s + 1) * P], sin[q][0:P, s, :],
                                                   C["ident"][0:P, 0:P])
                last.then_inc(turned, 1)
                pe.wait_ge(turned_out, (2 * g + 2) if kind == 3 else g + 1)
                wait(pe, res_ready, g - 1)
                if kind != 3:
                    wait(pe, stats_done, g - 1)
                    nc.tensor.matmul(ps_flat[q][:, 0:W], C[Wt][:, :], zT[q][:, 0:W], start=True, stop=True)
                for s in range(SLOTS):
                    o = ps_out[q][0:P, s * D:(s + 1) * D]
                    if kind != 3:
                        last = nc.tensor.matmul(o, zT[q][:, s * P:(s + 1) * P], C[Wt][:, :], start=True, stop=True)
                    else:
                        nc.tensor.matmul(o, zT[q][:, s * P:(s + 1) * P], C["Wc_x"][:, :], start=True, stop=False)
                        nc.tensor.matmul(o, sT[q][:, s * P:(s + 1) * P], C["Wc_a"][:, :], start=False, stop=False)
                        last = nc.tensor.matmul(o, C["one_row"][:, 0:P], C["bc_row"][:, :], start=False, stop=True)
                last.then_inc(mixed, 1)
            sweep(pe, NODE_FULL, NODE_TAIL, step)

        @block.scalar
        def _(act):
            def step(g, turn, q, P):
                W = P * SLOTS
                if kind == 3:
                    act.wait_ge(var_ready, g + 1)
                    nc.scalar.activation(sd[0:P, :], mv[0:P, :, 1], ACT.Sqrt, bias=C["eps"][0:P, :]).then_inc(sd_ready, 1)
                act.wait_ge(turned, g + 1)
                wait(act, mixed, g - 1)
                nc.scalar.copy(zT[q][:, 0:W], ps_zT[q][:, 0:W]).then_inc(turned_out, 1)
                if kind == 3:
                    nc.scalar.copy(sT[q][:, 0:W], ps_sT[q][:, 0:W]).then_inc(turned_out, 1)
                    act.wait_ge(mixed, g + 1)
                    wait(act, res_ready, g - 1)
                    nc.scalar.activation(h[q][0:P].rearrange("p s c -> p (s c)"), ps_out[q][0:P, :], ACT.Relu)\
                        .then_inc(h_ready, 1)
                    act.wait_ge(var2_ready, g + 1)
                    nc.scalar.activation(sd2[0:P, :], mv2[0:P, :, 1], ACT.Sqrt, bias=C["eps"][0:P, :]).then_inc(sd2_ready, 1)
                else:
                    act.wait_ge(mixed, g + 1)
                    wait(act, stored[q], DMA * turn)
                    if kind == 1:
                        act.wait_ge(dinv_ready, g + 1)
                    nc.scalar.copy(res[q][0:P, :, 0:D], ps_out[q][0:P, :].rearrange("p (s c) -> p s c", c=D))\
                        .then_inc(res_ready, 1)
            sweep(act, NODE_FULL, NODE_TAIL, step)


def norm_rows(nc, C, ph, first, bn_rows):
    with ExitStack() as ctx:
        one = lambda name, shape: ctx.enter_context(nc.sbuf_tensor(f"{ph}_{name}", shape, F32))
        mv = one("mv", [D, 2])
        sd = one("sd", [D, 1])
        ss = one("ss", [D, 2])
        mb = one("mb", [D, 1])
        wide = one("wide", [D, 2, 128])
        pr = ctx.enter_context(nc.psum_tensor(f"{ph}_ps", [128, 2 * D], F32))
        sem = lambda name: ctx.enter_context(nc.semaphore(f"{ph}_{name}"))
        chain_sem, var_ready, sd_ready, wide_ready, rows_ready = (sem(n) for n in ("chain", "var", "sd", "wide", "rows"))
        block = ctx.enter_context(nc.Block())
        b, gamma, beta = (C["vectors"][:, first + i:first + i + 1] for i in range(3))

        @block.vector
        def _(dve):
            ch = Chain(dve, chain_sem)
            ch.start(0)
            nc.vector.bn_aggr(mv[:, :], C["stats"][:, :]).then_inc(var_ready, 1)
            dve.wait_ge(sd_ready, 1)
            ch.link(nc.vector.reciprocal(sd[:, :], sd[:, :]))
            ch.link(nc.vector.tensor_tensor(mb[:, :], mv[:, 0:1], b, ALU.add))
            ch.link(nc.vector.tensor_tensor(ss[:, 0:1], gamma, sd[:, :], ALU.mult))
            ch.link(nc.vector.tensor_tensor(mb[:, :], b, mb[:, :], ALU.subtract))
            ch.link(nc.vector.tensor_tensor(mb[:, :], mb[:, :], ss[:, 0:1], ALU.mult))
            ch.link(nc.vector.tensor_tensor(ss[:, 1:2], mb[:, :], beta, ALU.add))
            nc.vector.tensor_copy(wide[:, :, :], ss[:, :].unsqueeze(2).to_broadcast([D, 2, 128])).then_inc(wide_ready, 1)
            dve.wait_ge(rows_ready, 1)
            nc.vector.tensor_copy(bn_rows[:, :, :], pr[:, :].rearrange("p (a c) -> p a c", a=2))

        @block.scalar
        def _(act):
            act.wait_ge(var_ready, 1)
            nc.scalar.activation(sd[:, :], mv[:, 1:2], ACT.Sqrt, bias=C["eps"][:, :]).then_inc(sd_ready, 1)

        @block.tensor
        def _(pe):
            pe.wait_ge(wide_ready, 1)
            for i in range(2):
                last = nc.tensor.matmul(pr[:, i * D:(i + 1) * D], wide[:, i, :], C["ident"][:, :], start=True, stop=True)
            last.then_inc(rows_ready, 1)


_INS = ["x", "src", "dst", "edge_weight", "L0_gnn_W1", "L0_gnn_b1", "L0_gnn_W2", "L0_gnn_b2", "L0_gnn_g1",
        "L0_gnn_beta1", "L0_gnn_g2", "L0_gnn_beta2", "L1_gnn_factors", "L1_gnn_Wm", "L1_gnn_bm", "L1_gnn_Wc",
        "L1_gnn_bc"]


def kernel(**inputs):
    import numpy as _np
    import concourse.bacc as _bacc
    from concourse import mybir as _mybir
    from concourse.bass_utils import run_bass_kernel_spmd as _run

    nc = _bacc.Bacc("TRN2", target_bir_lowering=False, num_devices=1)
    arrays, args = {}, []
    for name in _INS:
        a = _np.ascontiguousarray(inputs[name])
        arrays[f"in_{name}"] = a
        args.append(nc.dram_tensor(f"in_{name}", a.shape, _mybir.dt.from_np(a.dtype), kind="ExternalInput").ap())
    out = nc.dram_tensor("out_0", (N, D), F32, kind="ExternalOutput").ap()
    build(nc, *args, out)
    r = _run(nc, [arrays], core_ids=[0])
    return r.results[0]["out_0"]
```

```python
from contextlib import ExitStack

import concourse.bass as bass
from concourse import mybir

F32 = mybir.dt.float32
BF16 = mybir.dt.bfloat16
F16 = mybir.dt.float16
I32 = mybir.dt.int32
ALU = mybir.AluOpType
ACT = mybir.ActivationFunctionType

N = 100000
E = 50000
FACTORS = 50000
D = 128
SLOTS = 4
GROUP = 128 * SLOTS
EPS = 1e-5

NODE_FULL, NODE_TAIL = N // GROUP, (N % GROUP) // SLOTS
EDGE_FULL, EDGE_TAIL = E // GROUP, (E % GROUP) // SLOTS
NODE_GROUPS, EDGE_GROUPS = NODE_FULL + 1, EDGE_FULL + 1
DEG_COLS = NODE_GROUPS * SLOTS
ZERO_ROWS = -(-(N + GROUP) // EDGE_GROUPS)
ACC_ROWS = ZERO_ROWS * EDGE_GROUPS
assert D == 128
SEMAPHORES = 256
DMA = 16


def wait(eng, sem, value):
    if not isinstance(value, int) or value > 0:
        eng.wait_ge(sem, value)


def sweep(eng, full, tail, *stages, unroll=2):

    def position(turn, slot):
        for lag, step in stages:
            g = turn * unroll + slot - lag
            if not isinstance(g, int):
                step(g, turn + (slot - lag) // unroll, (slot - lag) % unroll, 128)
            elif 0 <= g <= full:
                step(g, g // unroll, g % unroll, tail if g == full else 128)

    first = 1 - -max(lag for lag, _ in stages) // unroll
    for g in range(first * unroll):
        position(g // unroll, g % unroll)
    with eng.Fori(first, full // unroll) as turn:
        for slot in range(unroll):
            position(turn, slot)
    for g in range(full // unroll * unroll, full + 1 + max(lag for lag, _ in stages)):
        position(g // unroll, g % unroll)


def wait_apart(eng, C, *waits):
    waits = [(sem, v) for sem, v in waits if not isinstance(v, int) or v > 0]
    for sem, value in waits:
        eng.wait_ge(sem, value)
    if waits:
        eng.sem_inc(C["passed"], 1)


class Chain:

    def __init__(self, eng, sem):
        self.eng, self.sem, self.base, self.n, self.per = eng, sem, 0, 0, None

    def start(self, group):
        self.base, self.n = group * (self.per or 0), 0

    def link(self, ins, apart=None):
        ins.then_inc(self.sem, 1)
        self.n += 1
        if apart is None:
            self.eng.wait_ge(self.sem, self.base + self.n)
        else:
            wait_apart(self.eng, apart, (self.sem, self.base + self.n))

    def end(self):
        self.per = self.per or self.n
        assert self.n == self.per, (self.n, self.per)


def zero_group(sums, group):
    rows = sums[bass.ds(group * ZERO_ROWS, ZERO_ROWS), :]
    return rows.rearrange("r c -> (r c)").rearrange("(p n) -> p n", p=128)


def row_groups(x, group, partitions):
    rows = x[bass.ds(group * GROUP, partitions * SLOTS), :]
    return rows.rearrange("(p s) c -> p s c", s=SLOTS)


def item_groups(x, group, partitions):
    return x[bass.ds(group * GROUP, partitions * SLOTS)].rearrange("(p s) -> p s", s=SLOTS)


def build(nc, x, src, dst, w, W1, b1, W2, b2, g1, beta1, g2, beta2, factors, Wm, bm, Wc, bc, out):
    top = ExitStack()
    with top:
        C = {}

        def keep(name, shape, dt=F32):
            C[name] = top.enter_context(nc.sbuf_tensor(name, shape, dt))
            return C[name]

        def dram(name, shape):
            return nc.dram_tensor(name, shape, F32).ap()

        table0 = dram("table0", (N, D + 1))
        table1 = dram("table1", (N, D + 1))
        table2 = dram("table2", (N, D))
        x_src = dram("x_src", (E, D))
        from_factor = dram("from_factor", (E, D))
        sums = [dram(f"sums{i}", (ACC_ROWS, D)) for i in range(3)]

        for name in ("ident", "W1", "W2", "Wm_i", "Wm_j", "Wc_x", "Wc_a"):
            keep(name, [128, 128])
        C["passed"] = top.enter_context(nc.semaphore("passed"))
        for ph, deep in (("d", 2), ("e1", 4), ("e2", 4), ("e3", 4)):
            C[f"{ph}_gathered"] = [top.enter_context(nc.semaphore(f"{ph}_gathered{q}")) for q in range(deep)]
            C[f"{ph}_scattered"] = last = top.enter_context(nc.semaphore(f"{ph}_scattered"))
        C["last_kept"] = last.num
        keep("ones3", [3, 128], BF16)
        keep("bm_rows", [128, D])
        keep("bc_rows", [3, D])
        keep("bc_parts", [3, GROUP], BF16)
        keep("vectors", [D, 6])
        keep("earlier", [128, SLOTS, GROUP])
        keep("spare", [128, SLOTS], I32)
        keep("iota", [128, DEG_COLS], F16)
        keep("zero", [128, ZERO_ROWS])
        keep("eps", [128, 1])
        keep("dinv", [128, DEG_COLS])
        keep("bn_rows1", [128, 2, D])
        keep("bn_rows2", [128, 2, D])
        keep("stats", [D, NODE_GROUPS * 6])

        setup(nc, C, W1, W2, Wm, Wc, bm, bc, (b1, g1, beta1, b2, g2, beta2))
        split_bc(nc, C)
        degrees(nc, C, dst, w, sums[0], factors, from_factor)
        with_dinv(nc, C, x, table0)
        edges(nc, C, "e1", 1, src, dst, w, table0, sums[0], sums[1], x_src, from_factor)
        nodes(nc, C, "n1", 1, x, x, sums[0], table1)
        norm_rows(nc, C, "m1", 0, C["bn_rows1"])
        edges(nc, C, "e2", 2, src, dst, w, table1, sums[1], sums[2], x_src, from_factor)
        nodes(nc, C, "n2", 2, x, table1, sums[1], table2)
        norm_rows(nc, C, "m2", 3, C["bn_rows2"])
        clear_semaphores(nc, C)
        edges(nc, C, "e3", 3, src, dst, w, table2, sums[2], None, x_src, from_factor)
        last_nodes(nc, C, x, table2, sums[2], out)


def setup(nc, C, W1, W2, Wm, Wc, bm, bc, vectors):
    with ExitStack() as ctx:
        loaded = ctx.enter_context(nc.semaphore("setup_loaded"))
        filled = ctx.enter_context(nc.semaphore("setup_filled"))
        block = ctx.enter_context(nc.Block())

        @block.sync
        def _(sp):
            n = 0
            for name, part in (("W1", W1), ("W2", W2), ("Wm_i", Wm[0:D, :]), ("Wm_j", Wm[D:2 * D, :]),
                               ("Wc_x", Wc[0:D, :]), ("Wc_a", Wc[D:2 * D, :])):
                sp.dma_start(C[name][:, :], part).then_inc(loaded, DMA)
                n += 1
            sp.dma_start(C["bc_rows"][:, :], bc.partition_broadcast(3)).then_inc(loaded, DMA)
            sp.dma_start(C["bm_rows"][:, :], bm.partition_broadcast(128)).then_inc(loaded, DMA)
            n += 2
            for i, v in enumerate(vectors):
                sp.dma_start(C["vectors"][:, i:i + 1], v.rearrange("(n o) -> n o", o=1)).then_inc(loaded, DMA)
                n += 1
            sp.wait_ge(loaded, DMA * n)

        @block.gpsimd
        def _(pool):
            pool.memset(C["ident"][:, :], 0.0).then_inc(filled, 1)
            pool.memset(C["earlier"][:, :, :], 1.0).then_inc(filled, 1)
            pool.iota(C["spare"][:, :], pattern=[[1, SLOTS]], base=N, channel_multiplier=SLOTS)
            pool.iota(C["iota"][:, :], pattern=[[1, DEG_COLS]], base=0, channel_multiplier=0,
                      allow_small_or_imprecise_dtypes=True)
            pool.wait_ge(filled, 2)
            pool.affine_select(out=C["ident"][:, :], in_=C["ident"][:, :], compare_op=ALU.not_equal, fill=1.0,
                               base=0, pattern=[[-1, 128]], channel_multiplier=1)
            for s in range(SLOTS):
                pool.affine_select(out=C["earlier"][:, s, :], in_=C["earlier"][:, s, :], compare_op=ALU.is_gt,
                                   fill=0.0, base=s, pattern=[[-1, GROUP]], channel_multiplier=SLOTS)

        @block.vector
        def _(dve):
            nc.vector.memset(C["ones3"][:, :], 1.0)
            nc.vector.memset(C["zero"][:, :], 0.0)
            nc.vector.memset(C["eps"][:, :], EPS)


def split_bc(nc, C):
    with ExitStack() as ctx:
        one = lambda name, dt=F32: ctx.enter_context(nc.sbuf_tensor(f"bc_{name}", [3, D], dt))
        part_b, part, rest, picked = one("part_b", BF16), one("part"), one("rest"), one("picked")
        chain_sem = ctx.enter_context(nc.semaphore("bc_chain"))
        block = ctx.enter_context(nc.Block())

        @block.vector
        def _(dve):
            ch = Chain(dve, chain_sem)
            left = C["bc_rows"]
            for k in range(3):
                ch.link(nc.vector.tensor_copy(part_b[:, :], left[:, :]))
                ch.link(nc.vector.tensor_copy(part[:, :], part_b[:, :]))
                if k < 2:
                    ch.link(nc.vector.tensor_tensor(rest[:, :], left[:, :], part[:, :], ALU.subtract))
                left = rest
                if k == 0:
                    ch.link(nc.vector.tensor_scalar(picked[:, :], part[:, :], C["ident"][0:3, k:k + 1], None, ALU.mult))
                else:
                    ch.link(nc.vector.scalar_tensor_tensor(picked[:, :], part[:, :], C["ident"][0:3, k:k + 1],
                                                           picked[:, :], ALU.mult, ALU.add))
            nc.vector.tensor_copy(C["bc_parts"][:, :].rearrange("p (s c) -> p s c", c=D),
                                  picked[:, :].unsqueeze(1).to_broadcast([3, SLOTS, D]))


def clear_semaphores(nc, C):
    with nc.Block() as block:
        @block.gpsimd
        def _(pool):
            pool.sem_clear(range(C["last_kept"] + 1, SEMAPHORES))


def degrees(nc, C, dst, w, sums, factors, from_factor):
    HALF = DEG_COLS // 2
    with ExitStack() as ctx:
        one = lambda name, shape, dt=F32: ctx.enter_context(nc.sbuf_tensor("d_" + name, shape, dt))
        sb = lambda name, shape, dt=F32: [one(f"{name}{q}", shape, dt) for q in range(2)]
        ps = lambda name: [ctx.enter_context(nc.psum_tensor(f"d_{name}{q}", [128, GROUP], F32)) for q in range(2)]
        sem = lambda name: ctx.enter_context(nc.semaphore("d_" + name))
        ids, ws = sb("ids", [128, SLOTS], I32), sb("ws", [128, SLOTS])
        fac_id, fac, facT = sb("fac_id", [128, SLOTS], I32), sb("fac", [128, SLOTS, D]), sb("facT", [128, GROUP])
        part = sb("part", [128, SLOTS, D])
        lo_i, hi_i = one("lo_i", [128, SLOTS], I32), one("hi_i", [128, SLOTS], I32)
        low2, col_i = one("low2", [128, SLOTS], I32), one("col_i", [128, SLOTS], I32)
        lo, col = one("lo", [128, SLOTS]), one("col", [128, SLOTS])
        part_b, rest = one("part_b", [128, SLOTS], BF16), one("rest", [128, SLOTS])
        parts = one("parts", [128, 3, SLOTS])
        hot_lo = sb("hot_lo", [128, SLOTS, 3, 128], BF16)
        hot_col = sb("hot_col", [128, SLOTS, DEG_COLS], BF16)
        zero_b = one("zero_b", [128, 512], BF16)
        positive, root = one("positive", [128, DEG_COLS]), one("root", [128, DEG_COLS])
        deg, ps_facT, ps_part = ps("deg"), ps("ps_facT"), ps("ps_part")
        loaded = [sem(f"loaded{q}") for q in range(2)]
        gathered = C["d_gathered"]
        stored = [sem(f"stored{q}") for q in range(2)]
        chain_sem, hot_ready, hot_used = sem("chain"), sem("hot_ready"), sem("hot_used")
        zero_ready, zeroed, rooted, clamped = sem("zero_ready"), sem("zeroed"), sem("rooted"), sem("clamped")
        fac_ready, turned, turned_out, mixed, part_ready = (
            sem(n) for n in ("fac_ready", "turned", "turned_out", "mixed", "part_ready"))
        block = ctx.enter_context(nc.Block())

        @block.sync
        def _(sp):
            def load(g, turn, q, P):
                wait(sp, hot_ready, g - 1)
                sp.dma_start(ids[q][0:P, :], item_groups(dst, g, P)).then_inc(loaded[q], DMA)
                sp.dma_start(ws[q][0:P, :], item_groups(w, g, P)).then_inc(loaded[q], DMA)
                sp.dma_start(zero_group(sums, g), C["zero"][:, :]).then_inc(zeroed, DMA)

            def store(g, turn, q, P):
                sp.wait_ge(part_ready, g + 1)
                sp.dma_start(row_groups(from_factor, g, P), part[q][0:P]).then_inc(stored[q], DMA)
            sweep(sp, EDGE_FULL, EDGE_TAIL, (0, load), (2, store))
            sp.wait_ge(zeroed, DMA * EDGE_GROUPS)
            for q in range(2):
                sp.wait_ge(stored[q], DMA * (EDGE_GROUPS // 2))

        @block.gpsimd
        def _(pool):
            def gather(g, turn, q, P):
                wait_apart(pool, C, (fac_ready, g + 1), (turned, g - 1))
                for s in range(SLOTS):
                    pool.indirect_dma_start(out=fac[q][0:P, s, :], out_offset=None, in_=factors,
                                            in_offset=bass.IndirectOffsetOnAxis(ap=fac_id[q][0:P, s:s + 1], axis=0))\
                        .then_inc(gathered[q], DMA)
            sweep(pool, EDGE_FULL, EDGE_TAIL, (0, gather))

        @block.scalar
        def _(act):
            def copy(g, turn, q, P):
                act.wait_ge(turned, g + 1)
                wait(act, mixed, g - 1)
                nc.scalar.copy(facT[q][:, 0:P * SLOTS], ps_facT[q][:, 0:P * SLOTS]).then_inc(turned_out, 1)
            sweep(act, EDGE_FULL, EDGE_TAIL, (0, copy))
            act.wait_ge(clamped, 1)
            nc.scalar.activation(root[:, :], C["dinv"][:, :], ACT.Sqrt).then_inc(rooted, 1)

        @block.vector
        def _(dve):
            ch = Chain(dve, chain_sem)
            nc.vector.memset(zero_b[:, :], 0.0).then_inc(zero_ready, 1)

            def hot(g, turn, q, P):
                ch.start(g)
                wait(dve, hot_ready, g)
                dve.wait_ge(loaded[q], 2 * DMA * turn + 2 * DMA)
                wait(dve, turned, g - 1)
                nc.vector.tensor_scalar(fac_id[q][0:P, :], ids[q][0:P, :], float(FACTORS - 1), None,
                                        ALU.min).then_inc(fac_ready, 1)
                nc.vector.tensor_scalar(lo_i[0:P, :], ids[q][0:P, :], 2, 127, ALU.logical_shift_right, ALU.bitwise_and)
                nc.vector.tensor_scalar(hi_i[0:P, :], ids[q][0:P, :], 9, 2, ALU.logical_shift_right, ALU.logical_shift_left)
                nc.vector.tensor_scalar(low2[0:P, :], ids[q][0:P, :], 3, None, ALU.bitwise_and)
                ch.link(nc.vector.tensor_copy(part_b[0:P, :], ws[q][0:P, :]))
                nc.vector.tensor_copy(parts[0:P, 0, :], part_b[0:P, :])
                ch.link(nc.vector.tensor_tensor(col_i[0:P, :], hi_i[0:P, :], low2[0:P, :], ALU.bitwise_or))
                nc.vector.tensor_copy(lo[0:P, :], lo_i[0:P, :])
                nc.vector.tensor_copy(col[0:P, :], col_i[0:P, :])
                ch.link(nc.vector.tensor_tensor(rest[0:P, :], ws[q][0:P, :], parts[0:P, 0, :], ALU.subtract))
                ch.link(nc.vector.tensor_copy(part_b[0:P, :], rest[0:P, :]))
                ch.link(nc.vector.tensor_copy(parts[0:P, 1, :], part_b[0:P, :]))
                ch.link(nc.vector.tensor_tensor(parts[0:P, 2, :], rest[0:P, :], parts[0:P, 1, :], ALU.subtract))
                wait(dve, hot_used, g - 1)
                for s in range(SLOTS):
                    nc.vector.tensor_scalar(hot_col[q][0:P, s, :], C["iota"][0:P, :], col[0:P, s:s + 1], None,
                                            ALU.is_equal)
                    for k in range(3):
                        last = nc.vector.tensor_scalar(hot_lo[q][0:P, s, k, :], C["iota"][0:P, 0:128], lo[0:P, s:s + 1],
                                                       parts[0:P, k, s:s + 1], ALU.is_equal, ALU.mult)
                last.then_inc(hot_ready, 1)
                ch.end()

            def add_bm(g, turn, q, P):
                dve.wait_ge(mixed, g + 1)
                wait(dve, stored[q], DMA * turn)
                nc.vector.tensor_tensor(part[q][0:P], ps_part[q][0:P, :].rearrange("p (s c) -> p s c", c=D),
                                        C["bm_rows"][0:P, :].unsqueeze(1).to_broadcast([P, SLOTS, D]), ALU.add)\
                    .then_inc(part_ready, 1)
            sweep(dve, EDGE_FULL, EDGE_TAIL, (0, hot), (1, add_bm))
            dve.wait_ge(hot_used, EDGE_GROUPS + 1)
            ch.start(EDGE_GROUPS)
            nc.vector.tensor_scalar(C["dinv"][:, 0:HALF], deg[0][:, 0:HALF], 1.0, None, ALU.add)
            ch.link(nc.vector.tensor_scalar(C["dinv"][:, HALF:], deg[1][:, 0:HALF], 1.0, None, ALU.add))
            ch.link(nc.vector.tensor_scalar(positive[:, :], C["dinv"][:, :], 0.0, None, ALU.is_gt))
            ch.link(nc.vector.scalar_tensor_tensor(C["dinv"][:, :], C["dinv"][:, :], 1.0, positive[:, :],
                                                   ALU.subtract, ALU.mult))
            ch.link(nc.vector.tensor_scalar(C["dinv"][:, :], C["dinv"][:, :], 1.0, None, ALU.add))
            nc.vector.memset(root[:, 0:1], 0.0).then_inc(clamped, 1)
            dve.wait_ge(rooted, 1)
            ch.link(nc.vector.reciprocal(root[:, :], root[:, :]))
            ch.link(nc.vector.tensor_tensor(C["dinv"][:, :], root[:, :], positive[:, :], ALU.mult))

        @block.tensor
        def _(pe):
            pe.wait_ge(zero_ready, 1)
            for i in range(2):
                nc.tensor.matmul(deg[i][:, 0:HALF], zero_b[:, 0:128], zero_b[:, 0:HALF], start=True, stop=False)

            def count(g, turn, q, P):
                pe.wait_ge(hot_ready, g + 1)
                for s in range(SLOTS):
                    for k in range(3):
                        for i in range(2):
                            last = nc.tensor.matmul(deg[i][:, 0:HALF], hot_lo[q][0:P, s, k, :],
                                                    hot_col[q][0:P, s, i * HALF:(i + 1) * HALF], start=False,
                                                    stop=False)
                last.then_inc(hot_used, 1)

            def turn_fac(g, turn, q, P):
                pe.wait_ge(gathered[q], SLOTS * DMA * turn + SLOTS * DMA)
                wait(pe, turned_out, g - 1)
                for s in range(SLOTS):
                    last = nc.tensor.transpose(ps_facT[q][:, s * P:(s + 1) * P], fac[q][0:P, s, :],
                                               C["ident"][0:P, 0:P])
                last.then_inc(turned, 1)

            def mix(g, turn, q, P):
                pe.wait_ge(turned_out, g + 1)
                wait(pe, part_ready, g - 1)
                for s in range(SLOTS):
                    last = nc.tensor.matmul(ps_part[q][0:P, s * D:(s + 1) * D], facT[q][:, s * P:(s + 1) * P],
                                            C["Wm_j"][:, :], start=True, stop=True)
                last.then_inc(mixed, 1)
            sweep(pe, EDGE_FULL, EDGE_TAIL, (1, mix), (0, turn_fac), (0, count))
            for i in range(2):
                last = nc.tensor.matmul(deg[i][:, 0:HALF], zero_b[:, 0:128], zero_b[:, 0:HALF], start=False, stop=True)
            last.then_inc(hot_used, 1)


def with_dinv(nc, C, x, table):
    DEEP = 4
    with ExitStack() as ctx:
        rows = [ctx.enter_context(nc.sbuf_tensor(f"s_rows{q}", [128, SLOTS, D + 1], F32)) for q in range(DEEP)]
        xin = [ctx.enter_context(nc.sbuf_tensor(f"s_x{q}", [128, SLOTS, D], F32)) for q in range(DEEP)]
        loaded = [ctx.enter_context(nc.semaphore(f"s_loaded{q}")) for q in range(DEEP)]
        stored = [ctx.enter_context(nc.semaphore(f"s_stored{q}")) for q in range(DEEP)]
        done = ctx.enter_context(nc.semaphore("s_done"))
        copied = ctx.enter_context(nc.semaphore("s_copied"))
        block = ctx.enter_context(nc.Block())

        @block.sync
        def _(sp):
            def load(g, turn, q, P):
                wait(sp, copied, g - DEEP + 1)
                sp.dma_start(xin[q][0:P], row_groups(x, g, P)).then_inc(loaded[q], DMA)
            sweep(sp, NODE_FULL, NODE_TAIL, (0, load), unroll=DEEP)

        @block.scalar
        def _(act):
            def store(g, turn, q, P):
                act.wait_ge(done, g + 1)
                act.wait_ge(copied, g + 1)
                act.dma_start(row_groups(table, g, P), rows[q][0:P]).then_inc(stored[q], DMA)
            sweep(act, NODE_FULL, NODE_TAIL, (0, store), unroll=DEEP)
            for q in range(DEEP):
                act.wait_ge(stored[q], DMA * len(range(q, NODE_GROUPS, DEEP)))

        @block.vector
        def _(dve):
            def fill(g, turn, q, P):
                wait_apart(dve, C, (stored[q], DMA * turn))
                nc.vector.tensor_copy(rows[q][0:P, :, D], C["dinv"][0:P, bass.ds(g * SLOTS, SLOTS)]).then_inc(done, 1)
                dve.wait_ge(loaded[q], DMA * turn + DMA)
                nc.vector.tensor_copy(rows[q][0:P, :, 0:D], xin[q][0:P]).then_inc(copied, 1)
            sweep(dve, NODE_FULL, NODE_TAIL, (0, fill), unroll=DEEP)


def edges(nc, C, ph, kind, src, dst, w, table, sums, next_sums, x_src, from_factor):
    cols = D if kind == 3 else D + 1
    key_of = src if kind == 3 else dst
    LOADS = 6 if kind == 3 else 4
    DEEP = 4
    with ExitStack() as ctx:
        one = lambda name, shape, dt=F32: ctx.enter_context(nc.sbuf_tensor(f"{ph}_{name}", shape, dt))
        sb = lambda name, shape, dt=F32: [one(f"{name}{q}", shape, dt) for q in range(DEEP)]
        ps = lambda name: [ctx.enter_context(nc.psum_tensor(f"{ph}_{name}{q}", [128, GROUP], F32)) for q in range(2)]
        sem = lambda name: ctx.enter_context(nc.semaphore(f"{ph}_{name}"))
        from_id, key = sb("from", [128, SLOTS], I32), sb("key", [128, SLOTS], I32)
        keys, wt = sb("keys", [128, GROUP], I32), sb("w", [128, SLOTS])
        rows = sb("rows", [128, SLOTS, cols])
        equal = sb("equal", [128, SLOTS, GROUP])
        add_at = sb("add_at", [128, SLOTS], I32)
        summed = sb("summed", [128, SLOTS, D])
        junk = one("junk", [128, SLOTS, GROUP], BF16)
        key_f = sb("key_f", [128, SLOTS])
        before, away, coef = (one(n, [128, SLOTS]) for n in ("before", "away", "coef"))
        ps_sum = ps("ps_sum")
        loaded = [sem(f"loaded{q}") for q in range(DEEP)]
        gathered, scattered = C[f"{ph}_gathered"], C[f"{ph}_scattered"]
        place_chain, equal_chain, equal_ready, rows_used = (
            sem(n) for n in ("place_chain", "equal_chain", "equal_ready", "rows_used"))
        combined, sum_ready, added_at = sem("combined"), sem("sum_ready"), sem("added_at")
        if kind == 1:
            kept = [sem(f"kept{q}") for q in range(DEEP)]
        if kind != 3:
            zeroed = sem("zeroed")
        if kind >= 2:
            msg = sb("msg", [128, SLOTS, D])
            msg_ready, norm_chain = sem("msg_ready"), sem("norm_chain")
        if kind == 3:
            xs, ff = sb("xs", [128, SLOTS, D]), sb("ff", [128, SLOTS, D])
            y = sb("y", [128, SLOTS, D])
            st, mv = sb("st", [128, SLOTS, 6]), sb("mv", [128, SLOTS, 2])
            scales_chain = sem("scales_chain")
            sd, rstd, shift_n = sb("sd", [128, SLOTS]), sb("rstd", [128, SLOTS]), sb("shift_n", [128, SLOTS])
            v, vT = sb("v", [128, SLOTS, D]), sb("vT", [128, GROUP])
            ps_vT, ps_msg = ps("ps_vT"), ps("ps_msg")
            var_ready, sd_ready, rstd_ready, v_ready = (sem(n) for n in ("var_ready", "sd_ready", "rstd_ready", "v_ready"))
            turned, turned_out, mixed = sem("turned"), sem("turned_out"), sem("mixed")
        bn = C["bn_rows2"] if kind == 3 else C["bn_rows1"]
        block = ctx.enter_context(nc.Block())

        @block.sync
        def _(sp):
            def load(g, turn, q, P):
                W = P * SLOTS
                wait(sp, equal_ready, g - DEEP + 1)
                if kind == 3:
                    wait(sp, rows_used, g - DEEP + 1)
                    wait(sp, mixed, g - DEEP + 1)
                sp.dma_start(from_id[q][0:P, :], item_groups(src, g, P)).then_inc(loaded[q], DMA)
                sp.dma_start(key[q][0:P, :], item_groups(key_of, g, P)).then_inc(loaded[q], DMA)
                sp.dma_start(wt[q][0:P, :], item_groups(w, g, P)).then_inc(loaded[q], DMA)
                sp.dma_start(keys[q][0:P, 0:W], key_of[bass.ds(g * GROUP, W)].partition_broadcast(P))\
                    .then_inc(loaded[q], DMA)
                if kind == 3:
                    sp.dma_start(xs[q][0:P], row_groups(x_src, g, P)).then_inc(loaded[q], DMA)
                    sp.dma_start(ff[q][0:P], row_groups(from_factor, g, P)).then_inc(loaded[q], DMA)
                if kind != 3:
                    sp.dma_start(zero_group(next_sums, g), C["zero"][:, :]).then_inc(zeroed, DMA)

            def keep_x(g, turn, q, P):
                sp.wait_ge(gathered[q], SLOTS * DMA * turn + SLOTS * DMA)
                sp.dma_start(row_groups(x_src, g, P), rows[q][0:P, :, 0:D]).then_inc(kept[q], DMA)
            sweep(sp, EDGE_FULL, EDGE_TAIL, (0, load), *([(3, keep_x)] if kind == 1 else []), unroll=DEEP)
            if kind != 3:
                sp.wait_ge(zeroed, DMA * EDGE_GROUPS)
            if kind == 1:
                for q in range(DEEP):
                    sp.wait_ge(kept[q], DMA * len(range(q, EDGE_GROUPS, DEEP)))

        @block.gpsimd
        def _(pool):
            def gather(g, turn, q, P):
                if kind == 1:
                    wait_apart(pool, C, (loaded[q], LOADS * DMA * turn + LOADS * DMA), (combined, g - DEEP + 1),
                               (kept[q], DMA * turn))
                else:
                    wait_apart(pool, C, (loaded[q], LOADS * DMA * turn + LOADS * DMA), (rows_used, g - DEEP + 1))
                for s in range(SLOTS):
                    pool.indirect_dma_start(out=rows[q][0:P, s, :], out_offset=None, in_=table,
                                            in_offset=bass.IndirectOffsetOnAxis(ap=from_id[q][0:P, s:s + 1], axis=0))\
                        .then_inc(gathered[q], DMA)

            def scatter(g, turn, q, P):
                wait_apart(pool, C, (sum_ready, g + 1), (added_at, g + 1), (scattered, DMA * SLOTS * g))
                for s in range(SLOTS):
                    pool.indirect_dma_start(out=sums, out_offset=bass.IndirectOffsetOnAxis(ap=add_at[q][0:P, s:s + 1], axis=0),
                                            in_=summed[q][0:P, s, :], in_offset=None, compute_op=ALU.add)\
                        .then_inc(scattered, DMA)
            sweep(pool, EDGE_FULL, EDGE_TAIL, (0, gather), (5 if kind == 3 else 2, scatter), unroll=DEEP)
            pool.wait_ge(scattered, DMA * SLOTS * EDGE_GROUPS)

        @block.vector
        def _(dve):
            ch_place, ch_equal = Chain(dve, place_chain), Chain(dve, equal_chain)

            def place(g, turn, q, P):
                W = P * SLOTS
                ch_place.start(g)
                wait(dve, added_at, g)
                dve.wait_ge(loaded[q], LOADS * DMA * turn + LOADS * DMA)
                nc.vector.tensor_copy(key_f[q][0:P, :], key[q][0:P, :])
                ch_place.link(nc.vector.tensor_tensor(away[0:P, :], C["spare"][0:P, :], key[q][0:P, :], ALU.subtract))
                for s in range(SLOTS):
                    last = nc.vector.scalar_tensor_tensor(junk[0:P, s, 0:W], keys[q][0:P, 0:W], key_f[q][0:P, s:s + 1],
                                                          C["earlier"][0:P, s, 0:W], ALU.is_equal, ALU.mult,
                                                          accum_out=before[0:P, s:s + 1])
                ch_place.link(last)
                ch_place.link(nc.vector.scalar_tensor_tensor(away[0:P, :], before[0:P, :], 0.0, away[0:P, :], ALU.is_gt,
                                                             ALU.mult))
                wait(dve, scattered, DMA * SLOTS * (g - DEEP + 1))
                nc.vector.tensor_tensor(add_at[q][0:P, :], away[0:P, :], key[q][0:P, :], ALU.add).then_inc(added_at, 1)
                ch_place.end()

            def equality(g, turn, q, P):
                W = P * SLOTS
                ch_equal.start(g)
                if kind != 3:
                    wait(dve, equal_ready, g)
                    dve.wait_ge(gathered[q], SLOTS * DMA * turn + SLOTS * DMA)
                    ch_equal.link(nc.vector.tensor_tensor(coef[0:P, :], wt[q][0:P, :], rows[q][0:P, :, D], ALU.mult))
                wait(dve, combined, g - DEEP + 1)
                for s in range(SLOTS):
                    last = nc.vector.tensor_scalar(equal[q][0:P, s, 0:W], keys[q][0:P, 0:W], key_f[q][0:P, s:s + 1],
                                                   None if kind == 3 else coef[0:P, s:s + 1], ALU.is_equal,
                                                   *(() if kind == 3 else (ALU.mult,)))
                last.then_inc(equal_ready, 1)
                ch_equal.end()

            if kind == 1:
                sweep(dve, EDGE_FULL, EDGE_TAIL, (0, place), (0, equality), unroll=DEEP)
                return
            ch_norm = Chain(dve, norm_chain)

            def norm(g, turn, q, P):
                to = msg[q][0:P] if kind == 2 else y[q][0:P]
                ch_norm.start(g)
                dve.wait_ge(gathered[q], SLOTS * DMA * turn + SLOTS * DMA)
                wait(dve, combined if kind == 2 else v_ready, g - DEEP + 1)
                ch_norm.link(nc.vector.tensor_tensor(to, rows[q][0:P, :, 0:D], bn[0:P, 0:1, :].to_broadcast([P, SLOTS, D]),
                                                     ALU.mult))
                ch_norm.link(nc.vector.tensor_tensor(to, to, bn[0:P, 1:2, :].to_broadcast([P, SLOTS, D]), ALU.add))
                if kind == 2:
                    nc.vector.tensor_scalar(to, to, 0.0, None, ALU.max).then_inc(rows_used, 1)
                    ch_norm.end()
                    return
                nc.vector.scalar_tensor_tensor(to, to, 0.0, xs[q][0:P], ALU.max, ALU.add).then_inc(rows_used, 1)
                dve.wait_ge(rows_used, g + 1)
                for s in range(SLOTS):
                    last = nc.vector.bn_stats(st[q][0:P, s, :], y[q][0:P, s, :])
                ch_norm.link(last, apart=C)
                for s in range(SLOTS):
                    last = nc.vector.bn_aggr(mv[q][0:P, s, :], st[q][0:P, s, :])
                last.then_inc(var_ready, 1)
                ch_norm.end()

            if kind == 2:
                sweep(dve, EDGE_FULL, EDGE_TAIL, (0, place), (0, equality), (0, norm), unroll=DEEP)
                return
            ch_scales = Chain(dve, scales_chain)

            def scales(g, turn, q, P):
                ch_scales.start(g)
                dve.wait_ge(sd_ready, g + 1)
                ch_scales.link(nc.vector.reciprocal(rstd[q][0:P, :], sd[q][0:P, :]))
                nc.vector.scalar_tensor_tensor(shift_n[q][0:P, :], mv[q][0:P, :, 0], -1.0, rstd[q][0:P, :], ALU.mult,
                                               ALU.mult).then_inc(rstd_ready, 1)
                ch_scales.end()
            sweep(dve, EDGE_FULL, EDGE_TAIL, (2, equality), (0, norm), (1, place), (0, scales), unroll=DEEP)

        @block.tensor
        def _(pe):
            def turn_v(g, turn, q, P):
                pe.wait_ge(v_ready, g + 1)
                wait(pe, turned_out, g - 1)
                for s in range(SLOTS):
                    last = nc.tensor.transpose(ps_vT[q % 2][:, s * P:(s + 1) * P], v[q][0:P, s, :], C["ident"][0:P, 0:P])
                last.then_inc(turned, 1)

            def mix(g, turn, q, P):
                pe.wait_ge(turned_out, g + 1)
                wait(pe, msg_ready, g - 1)
                for s in range(SLOTS):
                    o = ps_msg[q % 2][0:P, s * D:(s + 1) * D]
                    nc.tensor.matmul(o, C["ident"][0:P, 0:P], ff[q][0:P, s, :], start=True, stop=False)
                    last = nc.tensor.matmul(o, vT[q][:, s * P:(s + 1) * P], C["Wm_i"][:, :], start=False, stop=True)
                last.then_inc(mixed, 1)

            def combine(g, turn, q, P):
                if kind == 1:
                    pe.wait_ge(gathered[q], SLOTS * DMA * turn + SLOTS * DMA)
                    m_rows = rows[q]
                elif kind == 2:
                    pe.wait_ge(rows_used, g + 1)
                    m_rows = msg[q]
                else:
                    pe.wait_ge(msg_ready, g + 1)
                    m_rows = msg[q]
                pe.wait_ge(equal_ready, g + 1)
                wait(pe, sum_ready, g - 1)
                for m in range(SLOTS):
                    for s in range(SLOTS):
                        last = nc.tensor.matmul(ps_sum[q % 2][0:P, m * D:(m + 1) * D],
                                                equal[q][0:P, s, m:P * SLOTS:SLOTS], m_rows[0:P, s, 0:D],
                                                start=(s == 0), stop=(s == SLOTS - 1))
                last.then_inc(combined, 1)
            sweep(pe, EDGE_FULL, EDGE_TAIL, *([(0, turn_v), (1, combine), (0, mix)] if kind == 3 else [(0, combine)]),
                  unroll=DEEP)

        @block.scalar
        def _(act):
            def norm_v(g, turn, q, P):
                act.wait_ge(var_ready, g + 1)
                nc.scalar.activation(sd[q][0:P, :], mv[q][0:P, :, 1], ACT.Sqrt, bias=C["eps"][0:P, :]).then_inc(sd_ready, 1)
                act.wait_ge(rstd_ready, g + 1)
                wait(act, turned, g - DEEP + 1)
                for s in range(SLOTS):
                    last = nc.scalar.activation(v[q][0:P, s, :], y[q][0:P, s, :], ACT.Identity,
                                                bias=shift_n[q][0:P, s:s + 1], scale=rstd[q][0:P, s:s + 1])
                last.then_inc(v_ready, 1)

            def copy_v(g, turn, q, P):
                act.wait_ge(turned, g + 1)
                wait(act, mixed, g - DEEP + 1)
                nc.scalar.copy(vT[q][:, 0:P * SLOTS], ps_vT[q % 2][:, 0:P * SLOTS]).then_inc(turned_out, 1)

            def copy_msg(g, turn, q, P):
                act.wait_ge(mixed, g + 1)
                wait(act, combined, g - DEEP + 1)
                nc.scalar.activation(msg[q][0:P].rearrange("p s c -> p (s c)"), ps_msg[q % 2][0:P, :], ACT.Relu)\
                    .then_inc(msg_ready, 1)

            def copy_sum(g, turn, q, P):
                act.wait_ge(combined, g + 1)
                wait(act, scattered, DMA * SLOTS * (g - DEEP + 1))
                nc.scalar.copy(summed[q][0:P].rearrange("p s c -> p (s c)"), ps_sum[q % 2][0:P, :]).then_inc(sum_ready, 1)
            sweep(act, EDGE_FULL, EDGE_TAIL, *([(0, norm_v), (2, copy_sum), (1, copy_msg), (0, copy_v)] if kind == 3 else
                                               [(0, copy_sum)]), unroll=DEEP)


def nodes(nc, C, ph, kind, x, table, sums, out):
    DEEP = 4
    in_cols, out_cols = (D, D + 1) if kind == 1 else (D + 1, D)
    W_in = C["W1"] if kind == 1 else C["W2"]
    with ExitStack() as ctx:
        one = lambda name, shape, dt=F32: ctx.enter_context(nc.sbuf_tensor(f"{ph}_{name}", shape, dt))
        sb = lambda name, shape, dt=F32: [one(f"{name}{q}", shape, dt) for q in range(DEEP)]
        ps = lambda name: [ctx.enter_context(nc.psum_tensor(f"{ph}_{name}{q}", [128, GROUP], F32)) for q in range(2)]
        sem = lambda name: ctx.enter_context(nc.semaphore(f"{ph}_{name}"))
        rows, sin = sb("rows", [128, SLOTS, in_cols]), sb("sin", [128, SLOTS, D])
        a, z, res = sb("a", [128, SLOTS, D]), sb("z", [128, SLOTS, D]), sb("res", [128, SLOTS, out_cols])
        zT, hT = sb("zT", [128, GROUP]), sb("hT", [128, GROUP])
        ps_zT, ps_hT, ps_h = ps("ps_zT"), ps("ps_hT"), ps("ps_h")
        loaded = [sem(f"loaded{q}") for q in range(DEEP)]
        stored = [sem(f"stored{q}") for q in range(DEEP)]
        a_chain, z_chain, a_ready, z_ready, stats_done = (
            sem(n) for n in ("a_chain", "z_chain", "a_ready", "z_ready", "stats_done"))
        z_turned, z_copied, mixed, h_copied, h_turned, res_ready, dinv_ready = (
            sem(n) for n in ("z_turned", "z_copied", "mixed", "h_copied", "h_turned", "res_ready", "dinv_ready"))
        block = ctx.enter_context(nc.Block())

        def dinv_of(g, P):
            return C["dinv"][0:P, bass.ds(g * SLOTS, SLOTS)].unsqueeze(2).to_broadcast([P, SLOTS, D])

        @block.sync
        def _(sp):
            def load(g, turn, q, P):
                wait(sp, a_ready, g - DEEP + 1)
                wait(sp, z_ready, g - DEEP + 1)
                sp.dma_start(rows[q][0:P], row_groups(table, g, P)).then_inc(loaded[q], DMA)
                sp.dma_start(sin[q][0:P], row_groups(sums, g, P)).then_inc(loaded[q], DMA)

            def store(g, turn, q, P):
                sp.wait_ge(res_ready, g + 1)
                sp.dma_start(row_groups(out, g, P), res[q][0:P]).then_inc(stored[q], DMA)
            sweep(sp, NODE_FULL, NODE_TAIL, (0, load), (6, store), unroll=DEEP)
            for q in range(DEEP):
                sp.wait_ge(stored[q], DMA * len(range(q, NODE_GROUPS, DEEP)))

        @block.gpsimd
        def _(pool):
            ch = Chain(pool, a_chain)

            def first(g, turn, q, P):
                ch.start(g)
                pool.wait_ge(loaded[q], 2 * DMA * turn + 2 * DMA)
                wait(pool, z_ready, g - DEEP + 1)
                if kind == 1:
                    nc.gpsimd.tensor_tensor(a[q][0:P], rows[q][0:P], dinv_of(g, P), ALU.mult).then_inc(a_ready, 1)
                else:
                    ch.link(nc.gpsimd.tensor_tensor(a[q][0:P], rows[q][0:P, :, 0:D],
                                                    C["bn_rows1"][0:P, 0:1, :].to_broadcast([P, SLOTS, D]), ALU.mult))
                    nc.gpsimd.tensor_tensor(a[q][0:P], a[q][0:P],
                                            C["bn_rows1"][0:P, 1:2, :].to_broadcast([P, SLOTS, D]), ALU.add)\
                        .then_inc(a_ready, 1)
                ch.end()
            sweep(pool, NODE_FULL, NODE_TAIL, (0, first), unroll=DEEP)

        @block.vector
        def _(dve):
            ch = Chain(dve, z_chain)

            def to_z(g, turn, q, P):
                ch.start(g)
                dve.wait_ge(a_ready, g + 1)
                dve.wait_ge(loaded[q], 2 * DMA * turn + 2 * DMA)
                wait(dve, z_turned, g - DEEP + 1)
                left = a[q][0:P]
                if kind == 2:
                    ch.link(nc.vector.scalar_tensor_tensor(z[q][0:P], a[q][0:P], 0.0, dinv_of(g, P), ALU.max, ALU.mult))
                    left = z[q][0:P]
                ch.link(nc.vector.tensor_tensor(z[q][0:P], left, sin[q][0:P], ALU.add))
                nc.vector.tensor_tensor(z[q][0:P], z[q][0:P], dinv_of(g, P), ALU.mult).then_inc(z_ready, 1)
                ch.end()

            def stats(g, turn, q, P):
                dve.wait_ge(mixed, g + 1)
                nc.vector.bn_stats(C["stats"][:, bass.ds(g * 6, 6)], ps_hT[q % 2][:, 0:P * SLOTS]).then_inc(stats_done, 1)
                if kind == 1:
                    wait_apart(dve, C, (stored[q], DMA * turn))
                    nc.vector.tensor_copy(res[q][0:P, :, D], C["dinv"][0:P, bass.ds(g * SLOTS, SLOTS)])\
                        .then_inc(dinv_ready, 1)
            sweep(dve, NODE_FULL, NODE_TAIL, (0, to_z), (2, stats), unroll=DEEP)

        @block.tensor
        def _(pe):
            def mix(g, turn, q, P):
                pe.wait_ge(z_copied, g + 1)
                wait(pe, stats_done, g - 1)
                wait(pe, h_copied, g - 1)
                nc.tensor.matmul(ps_hT[q % 2][:, 0:P * SLOTS], W_in[:, :], zT[q][:, 0:P * SLOTS], start=True, stop=True)\
                    .then_inc(mixed, 1)

            def turn_z(g, turn, q, P):
                pe.wait_ge(z_ready, g + 1)
                wait(pe, z_copied, g - 1)
                for s in range(SLOTS):
                    last = nc.tensor.transpose(ps_zT[q % 2][:, s * P:(s + 1) * P], z[q][0:P, s, :], C["ident"][0:P, 0:P])
                last.then_inc(z_turned, 1)

            def turn_h(g, turn, q, P):
                pe.wait_ge(h_copied, g + 1)
                wait(pe, res_ready, g - 1)
                for s in range(SLOTS):
                    last = nc.tensor.transpose(ps_h[q % 2][0:P, s * D:(s + 1) * D], hT[q][:, s * P:(s + 1) * P],
                                               C["ident"][:, :])
                last.then_inc(h_turned, 1)
            sweep(pe, NODE_FULL, NODE_TAIL, (3, turn_h), (1, mix), (0, turn_z), unroll=DEEP)

        @block.scalar
        def _(act):
            def copy_h(g, turn, q, P):
                act.wait_ge(mixed, g + 1)
                act.wait_ge(stats_done, g + 1)
                wait(act, h_turned, g - DEEP + 1)
                nc.scalar.copy(hT[q][:, 0:P * SLOTS], ps_hT[q % 2][:, 0:P * SLOTS]).then_inc(h_copied, 1)

            def copy_z(g, turn, q, P):
                act.wait_ge(z_turned, g + 1)
                wait(act, mixed, g - DEEP + 1)
                nc.scalar.copy(zT[q][:, 0:P * SLOTS], ps_zT[q % 2][:, 0:P * SLOTS]).then_inc(z_copied, 1)

            def copy_rows(g, turn, q, P):
                act.wait_ge(h_turned, g + 1)
                if kind == 1:
                    act.wait_ge(dinv_ready, g + 1)
                wait(act, stored[q], DMA * turn)
                nc.scalar.copy(res[q][0:P, :, 0:D], ps_h[q % 2][0:P, :].rearrange("p (s c) -> p s c", c=D))\
                    .then_inc(res_ready, 1)
            sweep(act, NODE_FULL, NODE_TAIL, (3, copy_rows), (2, copy_h), (0, copy_z), unroll=DEEP)


def last_nodes(nc, C, x, table, sums, out):
    ph, DEEP = "n3", 4
    POOL_SLOTS = 3
    with ExitStack() as ctx:
        one = lambda name, shape, dt=F32: ctx.enter_context(nc.sbuf_tensor(f"{ph}_{name}", shape, dt))
        sb = lambda name, shape, dt=F32: [one(f"{name}{q}", shape, dt) for q in range(DEEP)]
        ps = lambda name, banks=1: [ctx.enter_context(nc.psum_tensor(f"{ph}_{name}{q}", [128, banks, GROUP], F32))
                                    for q in range(2)]
        sem = lambda name: ctx.enter_context(nc.semaphore(f"{ph}_{name}"))
        rows, sin, xin = (sb(n, [128, SLOTS, D]) for n in ("rows", "sin", "xin"))
        a, y, v, h, y2, res = (sb(n, [128, SLOTS, D]) for n in ("a", "y", "v", "h", "y2", "res"))
        both = sb("both", [128, 2, GROUP])
        st, st2 = sb("st", [128, SLOTS, 6]), sb("st2", [128, SLOTS, 6])
        mv, mv2 = sb("mv", [128, SLOTS, 2]), sb("mv2", [128, SLOTS, 2])
        sd, rstd, off, sd2, rstd2, off2 = (sb(n, [128, SLOTS]) for n in ("sd", "rstd", "off", "sd2", "rstd2", "off2"))
        ps_both, ps_out = ps("ps_both", 2), ps("ps_out")
        loaded = [sem(f"loaded{q}") for q in range(DEEP)]
        stored = [sem(f"stored{q}") for q in range(DEEP)]
        chain1, chain2, chain3, chain4, a_ready, y_ready, y2_ready = (
            sem(n) for n in ("chain1", "chain2", "chain3", "chain4", "a_ready", "y_ready", "y2_ready"))
        var, root, norm1, var2, root2, norm2 = (sem(n) for n in ("var", "root", "norm1", "var2", "root2", "norm2"))
        v_ready, turned, copied, mixed, h_ready, res_pool, res_act, pool_chain = (
            sem(n) for n in ("v_ready", "turned", "copied", "mixed", "h_ready", "res_pool", "res_act", "pool_chain"))
        block = ctx.enter_context(nc.Block())

        @block.sync
        def _(sp):
            def load(g, turn, q, P):
                wait(sp, y_ready, g - DEEP + 1)
                wait(sp, turned, g - DEEP + 1)
                sp.dma_start(rows[q][0:P], row_groups(table, g, P)).then_inc(loaded[q], DMA)
                sp.dma_start(sin[q][0:P], row_groups(sums, g, P)).then_inc(loaded[q], DMA)
                sp.dma_start(xin[q][0:P], row_groups(x, g, P)).then_inc(loaded[q], DMA)

            def store(g, turn, q, P):
                sp.wait_ge(res_pool, g + 1)
                sp.wait_ge(res_act, g + 1)
                sp.dma_start(row_groups(out, g, P), res[q][0:P]).then_inc(stored[q], DMA)
            sweep(sp, NODE_FULL, NODE_TAIL, (0, load), (9, store), unroll=DEEP)
            for q in range(DEEP):
                sp.wait_ge(stored[q], DMA * len(range(q, NODE_GROUPS, DEEP)))

        @block.gpsimd
        def _(pool):
            ch = Chain(pool, pool_chain)

            def scale(g, turn, q, P):
                ch.start(g)
                pool.wait_ge(loaded[q], 3 * DMA * turn + 3 * DMA)
                wait(pool, y_ready, g - DEEP + 1)
                ch.link(nc.gpsimd.tensor_tensor(a[q][0:P], rows[q][0:P],
                                                C["bn_rows2"][0:P, 0:1, :].to_broadcast([P, SLOTS, D]), ALU.mult))
                nc.gpsimd.tensor_tensor(a[q][0:P], a[q][0:P],
                                        C["bn_rows2"][0:P, 1:2, :].to_broadcast([P, SLOTS, D]), ALU.add)\
                    .then_inc(a_ready, 1)
                ch.end()

            def norm_out(g, turn, q, P):
                wait_apart(pool, C, (norm2, g + 1), (stored[q], DMA * turn))
                for s in range(POOL_SLOTS):
                    last = nc.gpsimd.tensor_scalar(res[q][0:P, s, :], y2[q][0:P, s, :], rstd2[q][0:P, s:s + 1],
                                                   off2[q][0:P, s:s + 1], ALU.mult, ALU.add)
                last.then_inc(res_pool, 1)
            sweep(pool, NODE_FULL, NODE_TAIL, (0, scale), (5, norm_out), unroll=DEEP)

        @block.vector
        def _(dve):
            ch1, ch2, ch3, ch4 = (Chain(dve, c) for c in (chain1, chain2, chain3, chain4))

            def to_y(g, turn, q, P):
                ch1.start(g)
                dve.wait_ge(a_ready, g + 1)
                dve.wait_ge(loaded[q], 3 * DMA * turn + 3 * DMA)
                wait(dve, v_ready, g - DEEP + 1)
                nc.vector.scalar_tensor_tensor(y[q][0:P], a[q][0:P], 0.0, xin[q][0:P], ALU.max, ALU.add)\
                    .then_inc(y_ready, 1)
                dve.wait_ge(y_ready, g + 1)
                for s in range(SLOTS):
                    last = nc.vector.bn_stats(st[q][0:P, s, :], y[q][0:P, s, :])
                ch1.link(last, apart=C)
                for s in range(SLOTS):
                    last = nc.vector.bn_aggr(mv[q][0:P, s, :], st[q][0:P, s, :])
                last.then_inc(var, 1)
                ch1.end()

            def to_y2(g, turn, q, P):
                ch2.start(g)
                dve.wait_ge(h_ready, g + 1)
                wait(dve, res_pool, g - DEEP + 1)
                wait(dve, res_act, g - DEEP + 1)
                nc.vector.scalar_tensor_tensor(y2[q][0:P], v[q][0:P], 2.0, h[q][0:P], ALU.mult, ALU.add)\
                    .then_inc(y2_ready, 1)
                dve.wait_ge(y2_ready, g + 1)
                for s in range(SLOTS):
                    last = nc.vector.bn_stats(st2[q][0:P, s, :], y2[q][0:P, s, :])
                ch2.link(last, apart=C)
                for s in range(SLOTS):
                    last = nc.vector.bn_aggr(mv2[q][0:P, s, :], st2[q][0:P, s, :])
                last.then_inc(var2, 1)
                ch2.end()

            def scales(g, turn, q, P):
                ch3.start(g)
                dve.wait_ge(root, g + 1)
                ch3.link(nc.vector.reciprocal(rstd[q][0:P, :], sd[q][0:P, :]))
                nc.vector.scalar_tensor_tensor(off[q][0:P, :], mv[q][0:P, :, 0], -1.0, rstd[q][0:P, :], ALU.mult,
                                               ALU.mult).then_inc(norm1, 1)
                ch3.end()

            def scales2(g, turn, q, P):
                ch4.start(g)
                dve.wait_ge(root2, g + 1)
                ch4.link(nc.vector.reciprocal(rstd2[q][0:P, :], sd2[q][0:P, :]))
                nc.vector.scalar_tensor_tensor(off2[q][0:P, :], mv2[q][0:P, :, 0], -1.0, rstd2[q][0:P, :], ALU.mult,
                                               ALU.mult).then_inc(norm2, 1)
                ch4.end()
            sweep(dve, NODE_FULL, NODE_TAIL, (5, scales2), (4, to_y2), (1, scales), (0, to_y), unroll=DEEP)

        @block.tensor
        def _(pe):
            def turn_both(g, turn, q, P):
                pe.wait_ge(v_ready, g + 1)
                pe.wait_ge(loaded[q], 3 * DMA * turn + 3 * DMA)
                wait(pe, copied, g - 1)
                for s in range(SLOTS):
                    nc.tensor.transpose(ps_both[q % 2][:, 0, s * P:(s + 1) * P], v[q][0:P, s, :], C["ident"][0:P, 0:P])
                for s in range(SLOTS):
                    last = nc.tensor.transpose(ps_both[q % 2][:, 1, s * P:(s + 1) * P], sin[q][0:P, s, :], C["ident"][0:P, 0:P])
                last.then_inc(turned, 1)

            def mix(g, turn, q, P):
                pe.wait_ge(copied, g + 1)
                wait(pe, h_ready, g - 1)
                nc.tensor.matmul(ps_out[q % 2][0:P, 0, :], C["ones3"][:, 0:P], C["bc_parts"][:, :], start=True, stop=False)
                for s in range(SLOTS):
                    o = ps_out[q % 2][0:P, 0, s * D:(s + 1) * D]
                    nc.tensor.matmul(o, both[q][:, 0, s * P:(s + 1) * P], C["Wc_x"][:, :], start=False, stop=False)
                    last = nc.tensor.matmul(o, both[q][:, 1, s * P:(s + 1) * P], C["Wc_a"][:, :], start=False,
                                            stop=s == SLOTS - 1)
                last.then_inc(mixed, 1)
            sweep(pe, NODE_FULL, NODE_TAIL, (1, mix), (0, turn_both), unroll=DEEP)

        @block.scalar
        def _(act):
            def relu(g, turn, q, P):
                act.wait_ge(mixed, g + 1)
                wait(act, y2_ready, g - DEEP + 1)
                nc.scalar.activation(h[q][0:P].rearrange("p s c -> p (s c)"), ps_out[q % 2][0:P, 0, :], ACT.Relu)\
                    .then_inc(h_ready, 1)

            def root1(g, turn, q, P):
                act.wait_ge(var, g + 1)
                nc.scalar.activation(sd[q][0:P, :], mv[q][0:P, :, 1], ACT.Sqrt, bias=C["eps"][0:P, :]).then_inc(root, 1)

            def root_2(g, turn, q, P):
                act.wait_ge(var2, g + 1)
                nc.scalar.activation(sd2[q][0:P, :], mv2[q][0:P, :, 1], ACT.Sqrt, bias=C["eps"][0:P, :]).then_inc(root2, 1)

            def norm_v(g, turn, q, P):
                act.wait_ge(norm1, g + 1)
                wait(act, turned, g - DEEP + 1)
                wait(act, y2_ready, g - DEEP + 1)
                for s in range(SLOTS):
                    last = nc.scalar.activation(v[q][0:P, s, :], y[q][0:P, s, :], ACT.Identity,
                                                bias=off[q][0:P, s:s + 1], scale=rstd[q][0:P, s:s + 1])
                last.then_inc(v_ready, 1)

            def copy(g, turn, q, P):
                act.wait_ge(turned, g + 1)
                wait(act, mixed, g - DEEP + 1)
                nc.scalar.copy(both[q][:, :, 0:P * SLOTS], ps_both[q % 2][:, :, 0:P * SLOTS]).then_inc(copied, 1)

            def norm_rest(g, turn, q, P):
                act.wait_ge(norm2, g + 1)
                wait(act, stored[q], DMA * turn)
                for s in range(POOL_SLOTS, SLOTS):
                    last = nc.scalar.activation(res[q][0:P, s, :], y2[q][0:P, s, :], ACT.Identity,
                                                bias=off2[q][0:P, s:s + 1], scale=rstd2[q][0:P, s:s + 1])
                last.then_inc(res_act, 1)
            sweep(act, NODE_FULL, NODE_TAIL, (3, relu), (2, copy), (1, norm_v), (0, root1), (4, norm_rest),
                  (3, root_2), unroll=DEEP)


def norm_rows(nc, C, ph, first, bn_rows):
    with ExitStack() as ctx:
        one = lambda name, shape: ctx.enter_context(nc.sbuf_tensor(f"{ph}_{name}", shape, F32))
        mv = one("mv", [D, 2])
        sd = one("sd", [D, 1])
        ss = one("ss", [D, 2])
        mb = one("mb", [D, 1])
        wide = one("wide", [D, 2, 128])
        pr = ctx.enter_context(nc.psum_tensor(f"{ph}_ps", [128, 2 * D], F32))
        sem = lambda name: ctx.enter_context(nc.semaphore(f"{ph}_{name}"))
        chain_sem, var_ready, sd_ready, wide_ready, rows_ready = (sem(n) for n in ("chain", "var", "sd", "wide", "rows"))
        block = ctx.enter_context(nc.Block())
        b, gamma, beta = (C["vectors"][:, first + i:first + i + 1] for i in range(3))

        @block.vector
        def _(dve):
            ch = Chain(dve, chain_sem)
            ch.start(0)
            nc.vector.bn_aggr(mv[:, :], C["stats"][:, :]).then_inc(var_ready, 1)
            dve.wait_ge(sd_ready, 1)
            ch.link(nc.vector.reciprocal(sd[:, :], sd[:, :]))
            ch.link(nc.vector.tensor_tensor(mb[:, :], mv[:, 0:1], b, ALU.add))
            ch.link(nc.vector.tensor_tensor(ss[:, 0:1], gamma, sd[:, :], ALU.mult))
            ch.link(nc.vector.tensor_tensor(mb[:, :], b, mb[:, :], ALU.subtract))
            ch.link(nc.vector.tensor_tensor(mb[:, :], mb[:, :], ss[:, 0:1], ALU.mult))
            ch.link(nc.vector.tensor_tensor(ss[:, 1:2], mb[:, :], beta, ALU.add))
            nc.vector.tensor_copy(wide[:, :, :], ss[:, :].unsqueeze(2).to_broadcast([D, 2, 128])).then_inc(wide_ready, 1)
            dve.wait_ge(rows_ready, 1)
            nc.vector.tensor_copy(bn_rows[:, :, :], pr[:, :].rearrange("p (a c) -> p a c", a=2))

        @block.scalar
        def _(act):
            act.wait_ge(var_ready, 1)
            nc.scalar.activation(sd[:, :], mv[:, 1:2], ACT.Sqrt, bias=C["eps"][:, :]).then_inc(sd_ready, 1)

        @block.tensor
        def _(pe):
            pe.wait_ge(wide_ready, 1)
            for i in range(2):
                last = nc.tensor.matmul(pr[:, i * D:(i + 1) * D], wide[:, i, :], C["ident"][:, :], start=True, stop=True)
            last.then_inc(rows_ready, 1)


_INS = ["x", "src", "dst", "edge_weight", "L0_gnn_W1", "L0_gnn_b1", "L0_gnn_W2", "L0_gnn_b2", "L0_gnn_g1",
        "L0_gnn_beta1", "L0_gnn_g2", "L0_gnn_beta2", "L1_gnn_factors", "L1_gnn_Wm", "L1_gnn_bm", "L1_gnn_Wc",
        "L1_gnn_bc"]


def kernel(**inputs):
    import numpy as _np
    import concourse.bacc as _bacc
    from concourse import mybir as _mybir
    from concourse.bass_utils import run_bass_kernel_spmd as _run

    nc = _bacc.Bacc("TRN2", target_bir_lowering=False, num_devices=1)
    arrays, args = {}, []
    for name in _INS:
        a = _np.ascontiguousarray(inputs[name])
        arrays[f"in_{name}"] = a
        args.append(nc.dram_tensor(f"in_{name}", a.shape, _mybir.dt.from_np(a.dtype), kind="ExternalInput").ap())
    out = nc.dram_tensor("out_0", (N, D), F32, kind="ExternalOutput").ap()
    build(nc, *args, out)
    r = _run(nc, [arrays], core_ids=[0])
    return r.results[0]["out_0"]
```

```python
from contextlib import ExitStack

import concourse.bass as bass
from concourse import mybir

F32 = mybir.dt.float32
BF16 = mybir.dt.bfloat16
F16 = mybir.dt.float16
I32 = mybir.dt.int32
ALU = mybir.AluOpType
ACT = mybir.ActivationFunctionType

N = 100000
E = 50000
FACTORS = 50000
D = 128
SLOTS = 4
GROUP = 128 * SLOTS
EPS = 1e-5

NODE_FULL, NODE_TAIL = N // GROUP, (N % GROUP) // SLOTS
EDGE_FULL, EDGE_TAIL = E // GROUP, (E % GROUP) // SLOTS
NODE_GROUPS, EDGE_GROUPS = NODE_FULL + 1, EDGE_FULL + 1
DEG_COLS = NODE_GROUPS * SLOTS
ZERO_ROWS = -(-(N + GROUP) // EDGE_GROUPS)
ACC_ROWS = ZERO_ROWS * EDGE_GROUPS
assert D == 128
SEMAPHORES = 256
DMA = 16


def wait(eng, sem, value):
    if not isinstance(value, int) or value > 0:
        eng.wait_ge(sem, value)


def sweep(eng, full, tail, *stages, unroll=2):

    def position(turn, slot):
        for lag, step in stages:
            g = turn * unroll + slot - lag
            if not isinstance(g, int):
                step(g, turn + (slot - lag) // unroll, (slot - lag) % unroll, 128)
            elif 0 <= g <= full:
                step(g, g // unroll, g % unroll, tail if g == full else 128)

    first = 1 - -max(lag for lag, _ in stages) // unroll
    for g in range(first * unroll):
        position(g // unroll, g % unroll)
    with eng.Fori(first, full // unroll) as turn:
        for slot in range(unroll):
            position(turn, slot)
    for g in range(full // unroll * unroll, full + 1 + max(lag for lag, _ in stages)):
        position(g // unroll, g % unroll)


def wait_apart(eng, C, *waits):
    waits = [(sem, v) for sem, v in waits if not isinstance(v, int) or v > 0]
    for sem, value in waits:
        eng.wait_ge(sem, value)
    if waits:
        eng.sem_inc(C["passed"], 1)


class Chain:

    def __init__(self, eng, sem):
        self.eng, self.sem, self.base, self.n, self.per = eng, sem, 0, 0, None

    def start(self, group):
        self.base, self.n = group * (self.per or 0), 0

    def link(self, ins):
        ins.then_inc(self.sem, 1)
        self.n += 1
        self.eng.wait_ge(self.sem, self.base + self.n)

    def end(self):
        self.per = self.per or self.n
        assert self.n == self.per, (self.n, self.per)


def zero_group(sums, group):
    rows = sums[bass.ds(group * ZERO_ROWS, ZERO_ROWS), :]
    return rows.rearrange("r c -> (r c)").rearrange("(p n) -> p n", p=128)


def row_groups(x, group, partitions):
    rows = x[bass.ds(group * GROUP, partitions * SLOTS), :]
    return rows.rearrange("(p s) c -> p s c", s=SLOTS)


def item_groups(x, group, partitions):
    return x[bass.ds(group * GROUP, partitions * SLOTS)].rearrange("(p s) -> p s", s=SLOTS)


def build(nc, x, src, dst, w, W1, b1, W2, b2, g1, beta1, g2, beta2, factors, Wm, bm, Wc, bc, out):
    top = ExitStack()
    with top:
        C = {}

        def keep(name, shape, dt=F32):
            C[name] = top.enter_context(nc.sbuf_tensor(name, shape, dt))
            return C[name]

        def dram(name, shape):
            return nc.dram_tensor(name, shape, F32).ap()

        table0 = dram("table0", (N, D + 1))
        table1 = dram("table1", (N, D + 1))
        table2 = dram("table2", (N, D))
        x_src = dram("x_src", (E, D))
        from_factor = dram("from_factor", (E, D))
        sums = [dram(f"sums{i}", (ACC_ROWS, D)) for i in range(3)]

        for name in ("ident", "W1", "W2", "Wm_i", "Wm_j", "Wc_x", "Wc_a"):
            keep(name, [128, 128])
        C["passed"] = top.enter_context(nc.semaphore("passed"))
        C["scattered"], C["gathered"] = {}, {}
        for ph, deep in (("d", 2), ("e1", 4), ("e2", 4), ("e3", 4)):
            C["gathered"][ph] = [top.enter_context(nc.semaphore(f"{ph}_gathered{q}")) for q in range(deep)]
        for ph in ("e1", "e2", "e3"):
            C["scattered"][ph] = top.enter_context(nc.semaphore(f"{ph}_scattered"))
        C["last_kept"] = C["scattered"]["e3"].num
        keep("ones3", [3, 128], BF16)
        keep("bm_rows", [3, D])
        keep("bm_parts", [3, GROUP], BF16)
        keep("bc_rows", [3, D])
        keep("bc_parts", [3, GROUP], BF16)
        keep("vectors", [D, 6])
        keep("earlier", [128, SLOTS, GROUP])
        keep("spare", [128, SLOTS], I32)
        keep("iota", [128, DEG_COLS], F16)
        keep("zero", [128, ZERO_ROWS])
        keep("eps", [128, 1])
        keep("dinv", [128, DEG_COLS])
        keep("bn_rows1", [128, 2, D])
        keep("bn_rows2", [128, 2, D])
        keep("stats", [D, NODE_GROUPS * 6])

        setup(nc, C, W1, W2, Wm, Wc, bm, bc, (b1, g1, beta1, b2, g2, beta2))
        split_bias(nc, C, "bc")
        split_bias(nc, C, "bm")
        degrees(nc, C, dst, w, sums[0], factors, from_factor)
        with_dinv(nc, C, x, table0)
        edges(nc, C, "e1", 1, src, dst, w, table0, sums[0], sums[1], x_src, from_factor)
        nodes(nc, C, "n1", 1, x, x, sums[0], table1)
        norm_rows(nc, C, "m1", 0, C["bn_rows1"])
        edges(nc, C, "e2", 2, src, dst, w, table1, sums[1], sums[2], x_src, from_factor)
        nodes(nc, C, "n2", 2, x, table1, sums[1], table2)
        norm_rows(nc, C, "m2", 3, C["bn_rows2"])
        clear_semaphores(nc, C)
        edges(nc, C, "e3", 3, src, dst, w, table2, sums[2], None, x_src, from_factor)
        last_nodes(nc, C, x, table2, sums[2], out)


def setup(nc, C, W1, W2, Wm, Wc, bm, bc, vectors):
    with ExitStack() as ctx:
        loaded = ctx.enter_context(nc.semaphore("setup_loaded"))
        filled = ctx.enter_context(nc.semaphore("setup_filled"))
        block = ctx.enter_context(nc.Block())

        @block.sync
        def _(sp):
            n = 0
            for name, part in (("W1", W1), ("W2", W2), ("Wm_i", Wm[0:D, :]), ("Wm_j", Wm[D:2 * D, :]),
                               ("Wc_x", Wc[0:D, :]), ("Wc_a", Wc[D:2 * D, :])):
                sp.dma_start(C[name][:, :], part).then_inc(loaded, DMA)
                n += 1
            sp.dma_start(C["bc_rows"][:, :], bc.partition_broadcast(3)).then_inc(loaded, DMA)
            sp.dma_start(C["bm_rows"][:, :], bm.partition_broadcast(3)).then_inc(loaded, DMA)
            n += 2
            for i, v in enumerate(vectors):
                sp.dma_start(C["vectors"][:, i:i + 1], v.rearrange("(n o) -> n o", o=1)).then_inc(loaded, DMA)
                n += 1
            sp.wait_ge(loaded, DMA * n)

        @block.gpsimd
        def _(pool):
            pool.memset(C["ident"][:, :], 0.0).then_inc(filled, 1)
            pool.memset(C["earlier"][:, :, :], 1.0).then_inc(filled, 1)
            pool.iota(C["spare"][:, :], pattern=[[1, SLOTS]], base=N, channel_multiplier=SLOTS)
            pool.iota(C["iota"][:, :], pattern=[[1, DEG_COLS]], base=0, channel_multiplier=0,
                      allow_small_or_imprecise_dtypes=True)
            pool.wait_ge(filled, 2)
            pool.affine_select(out=C["ident"][:, :], in_=C["ident"][:, :], compare_op=ALU.not_equal, fill=1.0,
                               base=0, pattern=[[-1, 128]], channel_multiplier=1)
            for s in range(SLOTS):
                pool.affine_select(out=C["earlier"][:, s, :], in_=C["earlier"][:, s, :], compare_op=ALU.is_gt,
                                   fill=0.0, base=s, pattern=[[-1, GROUP]], channel_multiplier=SLOTS)

        @block.vector
        def _(dve):
            nc.vector.memset(C["ones3"][:, :], 1.0)
            nc.vector.memset(C["zero"][:, :], 0.0)
            nc.vector.memset(C["eps"][:, :], EPS)


def split_bias(nc, C, name):
    with ExitStack() as ctx:
        one = lambda of, dt=F32: ctx.enter_context(nc.sbuf_tensor(f"{name}_{of}", [3, D], dt))
        part_b, part, rest, picked = one("part_b", BF16), one("part"), one("rest"), one("picked")
        chain_sem = ctx.enter_context(nc.semaphore(f"{name}_chain"))
        block = ctx.enter_context(nc.Block())

        @block.vector
        def _(dve):
            ch = Chain(dve, chain_sem)
            left = C[f"{name}_rows"]
            for k in range(3):
                ch.link(nc.vector.tensor_copy(part_b[:, :], left[:, :]))
                ch.link(nc.vector.tensor_copy(part[:, :], part_b[:, :]))
                if k < 2:
                    ch.link(nc.vector.tensor_tensor(rest[:, :], left[:, :], part[:, :], ALU.subtract))
                left = rest
                if k == 0:
                    ch.link(nc.vector.tensor_scalar(picked[:, :], part[:, :], C["ident"][0:3, k:k + 1], None, ALU.mult))
                else:
                    ch.link(nc.vector.scalar_tensor_tensor(picked[:, :], part[:, :], C["ident"][0:3, k:k + 1],
                                                           picked[:, :], ALU.mult, ALU.add))
            nc.vector.tensor_copy(C[f"{name}_parts"][:, :].rearrange("p (s c) -> p s c", c=D),
                                  picked[:, :].unsqueeze(1).to_broadcast([3, SLOTS, D]))


def clear_semaphores(nc, C):
    with nc.Block() as block:
        @block.gpsimd
        def _(pool):
            pool.sem_clear(range(C["last_kept"] + 1, SEMAPHORES))


def degrees(nc, C, dst, w, sums, factors, from_factor):
    HALF = DEG_COLS // 2
    PREP = 6
    with ExitStack() as ctx:
        one = lambda name, shape, dt=F32: ctx.enter_context(nc.sbuf_tensor("d_" + name, shape, dt))
        sb = lambda name, shape, dt=F32: [one(f"{name}{q}", shape, dt) for q in range(2)]
        ps = lambda name: [ctx.enter_context(nc.psum_tensor(f"d_{name}{q}", [128, GROUP], F32)) for q in range(2)]
        sem = lambda name: ctx.enter_context(nc.semaphore("d_" + name))
        ids, ws = sb("ids", [128, SLOTS], I32), sb("ws", [128, SLOTS])
        fac_id, fac, facT = sb("fac_id", [128, SLOTS], I32), sb("fac", [128, SLOTS, D]), sb("facT", [128, GROUP])
        part = sb("part", [128, SLOTS, D])
        lo_i, hi_i = one("lo_i", [128, SLOTS], I32), one("hi_i", [128, SLOTS], I32)
        low2, col_i = one("low2", [128, SLOTS], I32), one("col_i", [128, SLOTS], I32)
        lo, col, parts = sb("lo", [128, SLOTS]), sb("col", [128, SLOTS]), sb("parts", [128, 3, SLOTS])
        part_b, rest = one("part_b", [128, SLOTS], BF16), one("rest", [128, SLOTS])
        hot_lo = sb("hot_lo", [128, SLOTS, 3, 128], BF16)
        hot_col = sb("hot_col", [128, SLOTS, DEG_COLS], BF16)
        zero_b = one("zero_b", [128, 512], BF16)
        positive, root = one("positive", [128, DEG_COLS]), one("root", [128, DEG_COLS])
        deg, ps_facT, ps_part = ps("deg"), ps("ps_facT"), ps("ps_part")
        loaded = [sem(f"loaded{q}") for q in range(2)]
        gathered = C["gathered"]["d"]
        stored = [sem(f"stored{q}") for q in range(2)]
        chain_sem, prepared, hot_ready, hot_used = sem("chain"), sem("prepared"), sem("hot_ready"), sem("hot_used")
        zero_ready, zeroed, rooted, clamped = sem("zero_ready"), sem("zeroed"), sem("rooted"), sem("clamped")
        fac_ready, turned, turned_out, mixed, part_ready = (
            sem(n) for n in ("fac_ready", "turned", "turned_out", "mixed", "part_ready"))
        block = ctx.enter_context(nc.Block())

        @block.sync
        def _(sp):
            def load(g, turn, q, P):
                wait(sp, prepared, PREP * (g - 1))
                sp.dma_start(ids[q][0:P, :], item_groups(dst, g, P)).then_inc(loaded[q], DMA)
                sp.dma_start(ws[q][0:P, :], item_groups(w, g, P)).then_inc(loaded[q], DMA)
                sp.dma_start(zero_group(sums, g), C["zero"][:, :]).then_inc(zeroed, DMA)

            def store(g, turn, q, P):
                sp.wait_ge(part_ready, g + 1)
                sp.dma_start(row_groups(from_factor, g, P), part[q][0:P]).then_inc(stored[q], DMA)
            sweep(sp, EDGE_FULL, EDGE_TAIL, (0, load), (4, store))
            sp.wait_ge(zeroed, DMA * EDGE_GROUPS)
            for q in range(2):
                sp.wait_ge(stored[q], DMA * (EDGE_GROUPS // 2))

        @block.gpsimd
        def _(pool):
            def gather(g, turn, q, P):
                wait_apart(pool, C, (fac_ready, g + 1), (turned, g - 1))
                for s in range(SLOTS):
                    pool.indirect_dma_start(out=fac[q][0:P, s, :], out_offset=None, in_=factors,
                                            in_offset=bass.IndirectOffsetOnAxis(ap=fac_id[q][0:P, s:s + 1], axis=0))\
                        .then_inc(gathered[q], DMA)
            sweep(pool, EDGE_FULL, EDGE_TAIL, (0, gather))

        @block.scalar
        def _(act):
            def copy(g, turn, q, P):
                act.wait_ge(turned, g + 1)
                wait(act, mixed, g - 1)
                nc.scalar.copy(facT[q][:, 0:P * SLOTS], ps_facT[q][:, 0:P * SLOTS]).then_inc(turned_out, 1)

            def copy_part(g, turn, q, P):
                act.wait_ge(mixed, g + 1)
                wait(act, stored[q], DMA * turn)
                nc.scalar.copy(part[q][0:P], ps_part[q][0:P, :].rearrange("p (s c) -> p s c", c=D)).then_inc(part_ready, 1)
            sweep(act, EDGE_FULL, EDGE_TAIL, (1, copy_part), (0, copy))
            act.wait_ge(clamped, 1)
            nc.scalar.activation(root[:, :], C["dinv"][:, :], ACT.Sqrt).then_inc(rooted, 1)

        @block.vector
        def _(dve):
            ch = Chain(dve, chain_sem)
            nc.vector.memset(zero_b[:, :], 0.0).then_inc(zero_ready, 1)


            def read_ids(g, turn, q, P):
                dve.wait_ge(loaded[q], 2 * DMA * turn + 2 * DMA)
                wait(dve, prepared, PREP * g)
                wait(dve, turned, g - 1)
                nc.vector.tensor_scalar(fac_id[q][0:P, :], ids[q][0:P, :], float(FACTORS - 1), None,
                                        ALU.min).then_inc(fac_ready, 1)
                nc.vector.tensor_scalar(lo_i[0:P, :], ids[q][0:P, :], 2, 127, ALU.logical_shift_right, ALU.bitwise_and)
                nc.vector.tensor_scalar(hi_i[0:P, :], ids[q][0:P, :], 9, 2, ALU.logical_shift_right, ALU.logical_shift_left)
                nc.vector.tensor_scalar(low2[0:P, :], ids[q][0:P, :], 3, None, ALU.bitwise_and)
                nc.vector.tensor_copy(part_b[0:P, :], ws[q][0:P, :]).then_inc(prepared, 1)

            def first_part(g, turn, q, P):
                dve.wait_ge(prepared, PREP * g + 1)
                wait(dve, hot_ready, g - 1)
                nc.vector.tensor_copy(parts[q][0:P, 0, :], part_b[0:P, :])
                nc.vector.tensor_tensor(col_i[0:P, :], hi_i[0:P, :], low2[0:P, :], ALU.bitwise_or)
                nc.vector.tensor_copy(lo[q][0:P, :], lo_i[0:P, :]).then_inc(prepared, 1)

            def rest_of_w(g, turn, q, P):
                dve.wait_ge(prepared, PREP * g + 2)
                nc.vector.tensor_copy(col[q][0:P, :], col_i[0:P, :])
                nc.vector.tensor_tensor(rest[0:P, :], ws[q][0:P, :], parts[q][0:P, 0, :], ALU.subtract)\
                    .then_inc(prepared, 1)

            def round_rest(g, turn, q, P):
                dve.wait_ge(prepared, PREP * g + 3)
                nc.vector.tensor_copy(part_b[0:P, :], rest[0:P, :]).then_inc(prepared, 1)

            def second_part(g, turn, q, P):
                dve.wait_ge(prepared, PREP * g + 4)
                nc.vector.tensor_copy(parts[q][0:P, 1, :], part_b[0:P, :]).then_inc(prepared, 1)

            def third_part(g, turn, q, P):
                dve.wait_ge(prepared, PREP * g + 5)
                nc.vector.tensor_tensor(parts[q][0:P, 2, :], rest[0:P, :], parts[q][0:P, 1, :], ALU.subtract)\
                    .then_inc(prepared, 1)

            def hot(s):
                def fill(g, turn, q, P):
                    if s == 0:
                        dve.wait_ge(prepared, PREP * g + PREP)
                        wait(dve, hot_used, g - 1)
                    nc.vector.tensor_scalar(hot_col[q][0:P, s, :], C["iota"][0:P, :], col[q][0:P, s:s + 1], None,
                                            ALU.is_equal)
                    for k in range(3):
                        last = nc.vector.tensor_scalar(hot_lo[q][0:P, s, k, :], C["iota"][0:P, 0:128],
                                                       lo[q][0:P, s:s + 1], parts[q][0:P, k, s:s + 1], ALU.is_equal,
                                                       ALU.mult)
                    if s == SLOTS - 1:
                        last.then_inc(hot_ready, 1)
                return fill
            sweep(dve, EDGE_FULL, EDGE_TAIL, (0, read_ids), (1, hot(0)), (0, first_part), (1, hot(1)), (0, rest_of_w),
                  (1, hot(2)), (0, round_rest), (1, hot(3)), (0, second_part), (0, third_part))
            dve.wait_ge(hot_used, EDGE_GROUPS + 1)
            ch.start(0)
            nc.vector.tensor_scalar(C["dinv"][:, 0:HALF], deg[0][:, 0:HALF], 1.0, None, ALU.add)
            ch.link(nc.vector.tensor_scalar(C["dinv"][:, HALF:], deg[1][:, 0:HALF], 1.0, None, ALU.add))
            ch.link(nc.vector.tensor_scalar(positive[:, :], C["dinv"][:, :], 0.0, None, ALU.is_gt))
            ch.link(nc.vector.scalar_tensor_tensor(C["dinv"][:, :], C["dinv"][:, :], 1.0, positive[:, :],
                                                   ALU.subtract, ALU.mult))
            ch.link(nc.vector.tensor_scalar(C["dinv"][:, :], C["dinv"][:, :], 1.0, None, ALU.add))
            nc.vector.memset(root[:, 0:1], 0.0).then_inc(clamped, 1)
            dve.wait_ge(rooted, 1)
            ch.link(nc.vector.reciprocal(root[:, :], root[:, :]))
            ch.link(nc.vector.tensor_tensor(C["dinv"][:, :], root[:, :], positive[:, :], ALU.mult))

        @block.tensor
        def _(pe):
            pe.wait_ge(zero_ready, 1)
            for i in range(2):
                nc.tensor.matmul(deg[i][:, 0:HALF], zero_b[:, 0:128], zero_b[:, 0:HALF], start=True, stop=False)

            def count(g, turn, q, P):
                pe.wait_ge(hot_ready, g + 1)
                for s in range(SLOTS):
                    for k in range(3):
                        for i in range(2):
                            last = nc.tensor.matmul(deg[i][:, 0:HALF], hot_lo[q][0:P, s, k, :],
                                                    hot_col[q][0:P, s, i * HALF:(i + 1) * HALF], start=False,
                                                    stop=False)
                last.then_inc(hot_used, 1)

            def turn_fac(g, turn, q, P):
                pe.wait_ge(gathered[q], SLOTS * DMA * turn + SLOTS * DMA)
                wait(pe, turned_out, g - 1)
                for s in range(SLOTS):
                    last = nc.tensor.transpose(ps_facT[q][:, s * P:(s + 1) * P], fac[q][0:P, s, :],
                                               C["ident"][0:P, 0:P])
                last.then_inc(turned, 1)

            def mix(g, turn, q, P):
                pe.wait_ge(turned_out, g + 1)
                wait(pe, part_ready, g - 1)
                nc.tensor.matmul(ps_part[q][0:P, :], C["ones3"][:, 0:P], C["bm_parts"][:, :], start=True, stop=False)
                for s in range(SLOTS):
                    last = nc.tensor.matmul(ps_part[q][0:P, s * D:(s + 1) * D], facT[q][:, s * P:(s + 1) * P],
                                            C["Wm_j"][:, :], start=False, stop=s == SLOTS - 1)
                last.then_inc(mixed, 1)
            sweep(pe, EDGE_FULL, EDGE_TAIL, (0, turn_fac), (0, count), (1, mix))
            for i in range(2):
                last = nc.tensor.matmul(deg[i][:, 0:HALF], zero_b[:, 0:128], zero_b[:, 0:HALF], start=False, stop=True)
            last.then_inc(hot_used, 1)


def with_dinv(nc, C, x, table):
    DEEP = 4
    with ExitStack() as ctx:
        rows = [ctx.enter_context(nc.sbuf_tensor(f"s_rows{q}", [128, SLOTS, D + 1], F32)) for q in range(DEEP)]
        xin = [ctx.enter_context(nc.sbuf_tensor(f"s_x{q}", [128, SLOTS, D], F32)) for q in range(DEEP)]
        loaded = [ctx.enter_context(nc.semaphore(f"s_loaded{q}")) for q in range(DEEP)]
        stored = [ctx.enter_context(nc.semaphore(f"s_stored{q}")) for q in range(DEEP)]
        done = ctx.enter_context(nc.semaphore("s_done"))
        copied = ctx.enter_context(nc.semaphore("s_copied"))
        block = ctx.enter_context(nc.Block())

        @block.sync
        def _(sp):
            def load(g, turn, q, P):
                wait(sp, copied, g - DEEP + 1)
                sp.dma_start(xin[q][0:P], row_groups(x, g, P)).then_inc(loaded[q], DMA)
            sweep(sp, NODE_FULL, NODE_TAIL, (0, load), unroll=DEEP)

        @block.scalar
        def _(act):
            def store(g, turn, q, P):
                act.wait_ge(done, g + 1)
                act.wait_ge(copied, g + 1)
                act.dma_start(row_groups(table, g, P), rows[q][0:P]).then_inc(stored[q], DMA)
            sweep(act, NODE_FULL, NODE_TAIL, (0, store), unroll=DEEP)
            for q in range(DEEP):
                act.wait_ge(stored[q], DMA * len(range(q, NODE_GROUPS, DEEP)))

        @block.vector
        def _(dve):
            def fill(g, turn, q, P):
                wait_apart(dve, C, (stored[q], DMA * turn))
                nc.vector.tensor_copy(rows[q][0:P, :, D], C["dinv"][0:P, bass.ds(g * SLOTS, SLOTS)]).then_inc(done, 1)
                dve.wait_ge(loaded[q], DMA * turn + DMA)
                nc.vector.tensor_copy(rows[q][0:P, :, 0:D], xin[q][0:P]).then_inc(copied, 1)
            sweep(dve, NODE_FULL, NODE_TAIL, (0, fill), unroll=DEEP)


def edges(nc, C, ph, kind, src, dst, w, table, sums, next_sums, x_src, from_factor):
    cols = D if kind == 3 else D + 1
    key_of = src if kind == 3 else dst
    LOADS = 6 if kind == 3 else 4
    DEEP = 4
    with ExitStack() as ctx:
        one = lambda name, shape, dt=F32: ctx.enter_context(nc.sbuf_tensor(f"{ph}_{name}", shape, dt))
        sb = lambda name, shape, dt=F32: [one(f"{name}{q}", shape, dt) for q in range(DEEP)]
        ps = lambda name: [ctx.enter_context(nc.psum_tensor(f"{ph}_{name}{q}", [128, GROUP], F32)) for q in range(2)]
        sem = lambda name: ctx.enter_context(nc.semaphore(f"{ph}_{name}"))
        from_id, key = sb("from", [128, SLOTS], I32), sb("key", [128, SLOTS], I32)
        keys, wt = sb("keys", [128, GROUP], I32), sb("w", [128, SLOTS])
        rows = sb("rows", [128, SLOTS, cols])
        equal = sb("equal", [128, SLOTS, GROUP])
        add_at = sb("add_at", [128, SLOTS], I32)
        summed = sb("summed", [128, SLOTS, D])
        junk = one("junk", [128, SLOTS, GROUP], BF16)
        key_f, before, away = (sb(n, [128, SLOTS]) for n in ("key_f", "before", "away"))
        ps_sum = ps("ps_sum")
        loaded = [sem(f"loaded{q}") for q in range(DEEP)]
        gathered, scattered = C["gathered"][ph], C["scattered"][ph]
        key_ready, before_ready, away_ready, equal_ready = (
            sem(n) for n in ("key_ready", "before_ready", "away_ready", "equal_ready"))
        combined, sum_ready, added_at = sem("combined"), sem("sum_ready"), sem("added_at")
        if kind == 1:
            kept = [sem(f"kept{q}") for q in range(DEEP)]
        if kind != 3:
            coef = sb("coef", [128, SLOTS])
            zeroed, coef_ready = sem("zeroed"), sem("coef_ready")
        if kind >= 2:
            msg = sb("msg", [128, SLOTS, D])
            normed = msg
            scaled, shifted, rows_used = sem("scaled"), sem("shifted"), sem("rows_used")
        if kind == 3:
            xs, ff = sb("xs", [128, SLOTS, D]), sb("ff", [128, SLOTS, D])
            y = sb("y", [128, SLOTS, D])
            st, mv = sb("st", [128, SLOTS, 6]), sb("mv", [128, SLOTS, 2])
            normed, msg_ready = y, sem("msg_ready")
            st_ready, inverse_ready = sem("st_ready"), sem("inverse_ready")
            sd, rstd, shift_n = sb("sd", [128, SLOTS]), sb("rstd", [128, SLOTS]), sb("shift_n", [128, SLOTS])
            v, vT = sb("v", [128, SLOTS, D]), sb("vT", [128, GROUP])
            ps_vT, ps_msg = ps("ps_vT"), ps("ps_msg")
            var_ready, sd_ready, rstd_ready, v_ready = (sem(n) for n in ("var_ready", "sd_ready", "rstd_ready", "v_ready"))
            turned, turned_out, mixed = sem("turned"), sem("turned_out"), sem("mixed")
        bn = C["bn_rows2"] if kind == 3 else C["bn_rows1"]
        block = ctx.enter_context(nc.Block())

        @block.sync
        def _(sp):
            def load(g, turn, q, P):
                W = P * SLOTS
                wait(sp, equal_ready, g - DEEP + 1)
                wait(sp, added_at, g - DEEP + 1)
                if kind == 3:
                    wait(sp, rows_used, g - DEEP + 1)
                    wait(sp, mixed, g - DEEP + 1)
                sp.dma_start(from_id[q][0:P, :], item_groups(src, g, P)).then_inc(loaded[q], DMA)
                sp.dma_start(key[q][0:P, :], item_groups(key_of, g, P)).then_inc(loaded[q], DMA)
                sp.dma_start(wt[q][0:P, :], item_groups(w, g, P)).then_inc(loaded[q], DMA)
                sp.dma_start(keys[q][0:P, 0:W], key_of[bass.ds(g * GROUP, W)].partition_broadcast(P))\
                    .then_inc(loaded[q], DMA)
                if kind == 3:
                    sp.dma_start(xs[q][0:P], row_groups(x_src, g, P)).then_inc(loaded[q], DMA)
                    sp.dma_start(ff[q][0:P], row_groups(from_factor, g, P)).then_inc(loaded[q], DMA)
                if kind != 3:
                    sp.dma_start(zero_group(next_sums, g), C["zero"][:, :]).then_inc(zeroed, DMA)

            def keep_x(g, turn, q, P):
                sp.wait_ge(gathered[q], SLOTS * DMA * turn + SLOTS * DMA)
                sp.dma_start(row_groups(x_src, g, P), rows[q][0:P, :, 0:D]).then_inc(kept[q], DMA)
            sweep(sp, EDGE_FULL, EDGE_TAIL, (0, load), *([(3, keep_x)] if kind == 1 else []), unroll=DEEP)
            if kind != 3:
                sp.wait_ge(zeroed, DMA * EDGE_GROUPS)
            if kind == 1:
                for q in range(DEEP):
                    sp.wait_ge(kept[q], DMA * len(range(q, EDGE_GROUPS, DEEP)))

        @block.gpsimd
        def _(pool):
            def gather(g, turn, q, P):
                if kind == 1:
                    wait_apart(pool, C, (loaded[q], LOADS * DMA * turn + LOADS * DMA), (combined, g - DEEP + 1),
                               (kept[q], DMA * turn))
                else:
                    wait_apart(pool, C, (loaded[q], LOADS * DMA * turn + LOADS * DMA), (rows_used, g - DEEP + 1))
                for s in range(SLOTS):
                    pool.indirect_dma_start(out=rows[q][0:P, s, :], out_offset=None, in_=table,
                                            in_offset=bass.IndirectOffsetOnAxis(ap=from_id[q][0:P, s:s + 1], axis=0))\
                        .then_inc(gathered[q], DMA)

            def scatter(g, turn, q, P):
                wait_apart(pool, C, (sum_ready, g + 1), (added_at, g + 1), (scattered, DMA * SLOTS * g))
                for s in range(SLOTS):
                    pool.indirect_dma_start(out=sums, out_offset=bass.IndirectOffsetOnAxis(ap=add_at[q][0:P, s:s + 1], axis=0),
                                            in_=summed[q][0:P, s, :], in_offset=None, compute_op=ALU.add)\
                        .then_inc(scattered, DMA)
            sweep(pool, EDGE_FULL, EDGE_TAIL, (0, gather), (5 if kind == 3 else 2, scatter), unroll=DEEP)
            pool.wait_ge(scattered, DMA * SLOTS * EDGE_GROUPS)

        @block.vector
        def _(dve):
            def float_key(g, turn, q, P):
                dve.wait_ge(loaded[q], LOADS * DMA * turn + LOADS * DMA)
                wait(dve, added_at, g - DEEP + 1)
                wait(dve, equal_ready, g - DEEP + 1)
                nc.vector.tensor_copy(key_f[q][0:P, :], key[q][0:P, :])
                nc.vector.tensor_tensor(away[q][0:P, :], C["spare"][0:P, :], key[q][0:P, :], ALU.subtract)\
                    .then_inc(key_ready, 1)

            def count_before(g, turn, q, P):
                W = P * SLOTS
                dve.wait_ge(key_ready, g + 1)
                wait(dve, before_ready, g)
                for s in range(SLOTS):
                    last = nc.vector.scalar_tensor_tensor(junk[0:P, s, 0:W], keys[q][0:P, 0:W], key_f[q][0:P, s:s + 1],
                                                          C["earlier"][0:P, s, 0:W], ALU.is_equal, ALU.mult,
                                                          accum_out=before[q][0:P, s:s + 1])
                last.then_inc(before_ready, 1)

            def keep_away(g, turn, q, P):
                dve.wait_ge(before_ready, g + 1)
                nc.vector.scalar_tensor_tensor(away[q][0:P, :], before[q][0:P, :], 0.0, away[q][0:P, :], ALU.is_gt,
                                               ALU.mult).then_inc(away_ready, 1)

            def place(g, turn, q, P):
                dve.wait_ge(away_ready, g + 1)
                wait(dve, scattered, DMA * SLOTS * (g - DEEP + 1))
                nc.vector.tensor_tensor(add_at[q][0:P, :], away[q][0:P, :], key[q][0:P, :], ALU.add).then_inc(added_at, 1)

            def coefficient(g, turn, q, P):
                dve.wait_ge(gathered[q], SLOTS * DMA * turn + SLOTS * DMA)
                wait(dve, equal_ready, g - DEEP + 1)
                nc.vector.tensor_tensor(coef[q][0:P, :], wt[q][0:P, :], rows[q][0:P, :, D], ALU.mult)\
                    .then_inc(coef_ready, 1)

            def equality(g, turn, q, P):
                W = P * SLOTS
                dve.wait_ge(key_ready, g + 1)
                if kind != 3:
                    dve.wait_ge(coef_ready, g + 1)
                wait(dve, combined, g - DEEP + 1)
                for s in range(SLOTS):
                    last = nc.vector.tensor_scalar(equal[q][0:P, s, 0:W], keys[q][0:P, 0:W], key_f[q][0:P, s:s + 1],
                                                   None if kind == 3 else coef[q][0:P, s:s + 1], ALU.is_equal,
                                                   *(() if kind == 3 else (ALU.mult,)))
                last.then_inc(equal_ready, 1)

            def scale_rows(g, turn, q, P):
                dve.wait_ge(gathered[q], SLOTS * DMA * turn + SLOTS * DMA)
                wait(dve, combined if kind == 2 else v_ready, g - DEEP + 1)
                nc.vector.tensor_tensor(normed[q][0:P], rows[q][0:P, :, 0:D], bn[0:P, 0:1, :].to_broadcast([P, SLOTS, D]),
                                        ALU.mult).then_inc(scaled, 1)

            def shift_rows(g, turn, q, P):
                dve.wait_ge(scaled, g + 1)
                nc.vector.tensor_tensor(normed[q][0:P], normed[q][0:P], bn[0:P, 1:2, :].to_broadcast([P, SLOTS, D]),
                                        ALU.add).then_inc(shifted, 1)

            def relu_rows(g, turn, q, P):
                dve.wait_ge(shifted, g + 1)
                if kind == 2:
                    nc.vector.tensor_scalar(normed[q][0:P], normed[q][0:P], 0.0, None, ALU.max).then_inc(rows_used, 1)
                else:
                    nc.vector.scalar_tensor_tensor(y[q][0:P], y[q][0:P], 0.0, xs[q][0:P], ALU.max, ALU.add)\
                        .then_inc(rows_used, 1)

            def stats(g, turn, q, P):
                dve.wait_ge(rows_used, g + 1)
                for s in range(SLOTS):
                    last = nc.vector.bn_stats(st[q][0:P, s, :], y[q][0:P, s, :])
                last.then_inc(st_ready, 1)

            def variance(g, turn, q, P):
                wait_apart(dve, C, (st_ready, g + 1))
                for s in range(SLOTS):
                    last = nc.vector.bn_aggr(mv[q][0:P, s, :], st[q][0:P, s, :])
                last.then_inc(var_ready, 1)

            def invert(g, turn, q, P):
                dve.wait_ge(sd_ready, g + 1)
                nc.vector.reciprocal(rstd[q][0:P, :], sd[q][0:P, :]).then_inc(inverse_ready, 1)

            def mean_shift(g, turn, q, P):
                dve.wait_ge(inverse_ready, g + 1)
                nc.vector.scalar_tensor_tensor(shift_n[q][0:P, :], mv[q][0:P, :, 0], -1.0, rstd[q][0:P, :], ALU.mult,
                                               ALU.mult).then_inc(rstd_ready, 1)
            steps = {
                1: [(0, float_key), (0, coefficient), (0, count_before), (0, equality), (0, keep_away), (0, place)],
                2: [(0, float_key), (0, scale_rows), (0, count_before), (0, shift_rows), (0, keep_away), (0, coefficient),
                    (0, relu_rows), (0, place), (0, equality)],
                3: [(0, scale_rows), (0, float_key), (0, shift_rows), (0, relu_rows), (0, count_before), (0, stats),
                    (0, variance), (1, equality), (0, invert), (0, keep_away), (1, place), (0, mean_shift)]}[kind]
            sweep(dve, EDGE_FULL, EDGE_TAIL, *steps, unroll=DEEP)

        @block.tensor
        def _(pe):
            def turn_v(g, turn, q, P):
                pe.wait_ge(v_ready, g + 1)
                wait(pe, turned_out, g - 1)
                for s in range(SLOTS):
                    last = nc.tensor.transpose(ps_vT[q % 2][:, s * P:(s + 1) * P], v[q][0:P, s, :], C["ident"][0:P, 0:P])
                last.then_inc(turned, 1)

            def mix(g, turn, q, P):
                pe.wait_ge(turned_out, g + 1)
                wait(pe, msg_ready, g - 1)
                for s in range(SLOTS):
                    o = ps_msg[q % 2][0:P, s * D:(s + 1) * D]
                    nc.tensor.matmul(o, C["ident"][0:P, 0:P], ff[q][0:P, s, :], start=True, stop=False)
                    last = nc.tensor.matmul(o, vT[q][:, s * P:(s + 1) * P], C["Wm_i"][:, :], start=False, stop=True)
                last.then_inc(mixed, 1)

            def combine(g, turn, q, P):
                if kind == 1:
                    pe.wait_ge(gathered[q], SLOTS * DMA * turn + SLOTS * DMA)
                    m_rows = rows[q]
                elif kind == 2:
                    pe.wait_ge(rows_used, g + 1)
                    m_rows = msg[q]
                else:
                    pe.wait_ge(msg_ready, g + 1)
                    m_rows = msg[q]
                pe.wait_ge(equal_ready, g + 1)
                wait(pe, sum_ready, g - 1)
                for m in range(SLOTS):
                    for s in range(SLOTS):
                        last = nc.tensor.matmul(ps_sum[q % 2][0:P, m * D:(m + 1) * D],
                                                equal[q][0:P, s, m:P * SLOTS:SLOTS], m_rows[0:P, s, 0:D],
                                                start=(s == 0), stop=(s == SLOTS - 1))
                last.then_inc(combined, 1)
            sweep(pe, EDGE_FULL, EDGE_TAIL, *([(0, turn_v), (0, mix), (0, combine)] if kind == 3 else [(0, combine)]),
                  unroll=DEEP)

        @block.scalar
        def _(act):
            def root(g, turn, q, P):
                act.wait_ge(var_ready, g + 1)
                nc.scalar.activation(sd[q][0:P, :], mv[q][0:P, :, 1], ACT.Sqrt, bias=C["eps"][0:P, :]).then_inc(sd_ready, 1)

            def norm_v(g, turn, q, P):
                act.wait_ge(rstd_ready, g + 1)
                wait(act, turned, g - DEEP + 1)
                for s in range(SLOTS):
                    last = nc.scalar.activation(v[q][0:P, s, :], y[q][0:P, s, :], ACT.Identity,
                                                bias=shift_n[q][0:P, s:s + 1], scale=rstd[q][0:P, s:s + 1])
                last.then_inc(v_ready, 1)

            def copy_v(g, turn, q, P):
                act.wait_ge(turned, g + 1)
                wait(act, mixed, g - DEEP + 1)
                nc.scalar.copy(vT[q][:, 0:P * SLOTS], ps_vT[q % 2][:, 0:P * SLOTS]).then_inc(turned_out, 1)

            def copy_msg(g, turn, q, P):
                act.wait_ge(mixed, g + 1)
                wait(act, combined, g - DEEP + 1)
                nc.scalar.activation(msg[q][0:P].rearrange("p s c -> p (s c)"), ps_msg[q % 2][0:P, :], ACT.Relu)\
                    .then_inc(msg_ready, 1)

            def copy_sum(g, turn, q, P):
                act.wait_ge(combined, g + 1)
                wait(act, scattered, DMA * SLOTS * (g - DEEP + 1))
                nc.scalar.copy(summed[q][0:P].rearrange("p s c -> p (s c)"), ps_sum[q % 2][0:P, :]).then_inc(sum_ready, 1)
            sweep(act, EDGE_FULL, EDGE_TAIL, *([(2, copy_sum), (0, root), (1, copy_msg), (0, norm_v), (0, copy_v)] if kind == 3 else
                                               [(0, copy_sum)]), unroll=DEEP)


def nodes(nc, C, ph, kind, x, table, sums, out):
    DEEP = 4
    in_cols, out_cols = (D, D + 1) if kind == 1 else (D + 1, D)
    W_in = C["W1"] if kind == 1 else C["W2"]
    with ExitStack() as ctx:
        one = lambda name, shape, dt=F32: ctx.enter_context(nc.sbuf_tensor(f"{ph}_{name}", shape, dt))
        sb = lambda name, shape, dt=F32: [one(f"{name}{q}", shape, dt) for q in range(DEEP)]
        ps = lambda name: [ctx.enter_context(nc.psum_tensor(f"{ph}_{name}{q}", [128, GROUP], F32)) for q in range(2)]
        sem = lambda name: ctx.enter_context(nc.semaphore(f"{ph}_{name}"))
        rows, sin = sb("rows", [128, SLOTS, in_cols]), sb("sin", [128, SLOTS, D])
        a, z, res = sb("a", [128, SLOTS, D]), sb("z", [128, SLOTS, D]), sb("res", [128, SLOTS, out_cols])
        zT, hT = sb("zT", [128, GROUP]), sb("hT", [128, GROUP])
        ps_zT, ps_hT, ps_h = ps("ps_zT"), ps("ps_hT"), ps("ps_h")
        loaded = [sem(f"loaded{q}") for q in range(DEEP)]
        stored = [sem(f"stored{q}") for q in range(DEEP)]
        a_chain, own_ready, z_summed, a_ready, z_ready, stats_done = (
            sem(n) for n in ("a_chain", "own_ready", "z_summed", "a_ready", "z_ready", "stats_done"))
        z_turned, z_copied, mixed, h_copied, h_turned, res_ready, dinv_ready = (
            sem(n) for n in ("z_turned", "z_copied", "mixed", "h_copied", "h_turned", "res_ready", "dinv_ready"))
        block = ctx.enter_context(nc.Block())

        def dinv_of(g, P):
            return C["dinv"][0:P, bass.ds(g * SLOTS, SLOTS)].unsqueeze(2).to_broadcast([P, SLOTS, D])

        @block.sync
        def _(sp):
            def load(g, turn, q, P):
                wait(sp, a_ready, g - DEEP + 1)
                wait(sp, z_ready, g - DEEP + 1)
                sp.dma_start(rows[q][0:P], row_groups(table, g, P)).then_inc(loaded[q], DMA)
                sp.dma_start(sin[q][0:P], row_groups(sums, g, P)).then_inc(loaded[q], DMA)

            def store(g, turn, q, P):
                sp.wait_ge(res_ready, g + 1)
                sp.dma_start(row_groups(out, g, P), res[q][0:P]).then_inc(stored[q], DMA)
            sweep(sp, NODE_FULL, NODE_TAIL, (0, load), (6, store), unroll=DEEP)
            for q in range(DEEP):
                sp.wait_ge(stored[q], DMA * len(range(q, NODE_GROUPS, DEEP)))

        @block.gpsimd
        def _(pool):
            ch = Chain(pool, a_chain)

            def first(g, turn, q, P):
                ch.start(g)
                pool.wait_ge(loaded[q], 2 * DMA * turn + 2 * DMA)
                wait(pool, z_ready, g - DEEP + 1)
                if kind == 1:
                    nc.gpsimd.tensor_tensor(a[q][0:P], rows[q][0:P], dinv_of(g, P), ALU.mult).then_inc(a_ready, 1)
                else:
                    ch.link(nc.gpsimd.tensor_tensor(a[q][0:P], rows[q][0:P, :, 0:D],
                                                    C["bn_rows1"][0:P, 0:1, :].to_broadcast([P, SLOTS, D]), ALU.mult))
                    nc.gpsimd.tensor_tensor(a[q][0:P], a[q][0:P],
                                            C["bn_rows1"][0:P, 1:2, :].to_broadcast([P, SLOTS, D]), ALU.add)\
                        .then_inc(a_ready, 1)
                ch.end()
            sweep(pool, NODE_FULL, NODE_TAIL, (0, first), unroll=DEEP)

        @block.vector
        def _(dve):
            def relu_dinv(g, turn, q, P):
                dve.wait_ge(a_ready, g + 1)
                wait(dve, z_turned, g - DEEP + 1)
                nc.vector.scalar_tensor_tensor(z[q][0:P], a[q][0:P], 0.0, dinv_of(g, P), ALU.max, ALU.mult)\
                    .then_inc(own_ready, 1)

            def add_sums(g, turn, q, P):
                dve.wait_ge(loaded[q], 2 * DMA * turn + 2 * DMA)
                if kind == 1:
                    dve.wait_ge(a_ready, g + 1)
                    wait(dve, z_turned, g - DEEP + 1)
                else:
                    dve.wait_ge(own_ready, g + 1)
                nc.vector.tensor_tensor(z[q][0:P], a[q][0:P] if kind == 1 else z[q][0:P], sin[q][0:P], ALU.add)\
                    .then_inc(z_summed, 1)

            def times_dinv(g, turn, q, P):
                dve.wait_ge(z_summed, g + 1)
                nc.vector.tensor_tensor(z[q][0:P], z[q][0:P], dinv_of(g, P), ALU.mult).then_inc(z_ready, 1)

            def stats(g, turn, q, P):
                dve.wait_ge(mixed, g + 1)
                nc.vector.bn_stats(C["stats"][:, bass.ds(g * 6, 6)], ps_hT[q % 2][:, 0:P * SLOTS]).then_inc(stats_done, 1)
                if kind == 1:
                    wait_apart(dve, C, (stored[q], DMA * turn))
                    nc.vector.tensor_copy(res[q][0:P, :, D], C["dinv"][0:P, bass.ds(g * SLOTS, SLOTS)])\
                        .then_inc(dinv_ready, 1)
            if kind == 1:
                sweep(dve, NODE_FULL, NODE_TAIL, (0, add_sums), (2, stats), (0, times_dinv), unroll=DEEP)
            else:
                sweep(dve, NODE_FULL, NODE_TAIL, (0, relu_dinv), (2, stats), (0, add_sums), (0, times_dinv), unroll=DEEP)

        @block.tensor
        def _(pe):
            def mix(g, turn, q, P):
                pe.wait_ge(z_copied, g + 1)
                wait(pe, stats_done, g - 1)
                wait(pe, h_copied, g - 1)
                nc.tensor.matmul(ps_hT[q % 2][:, 0:P * SLOTS], W_in[:, :], zT[q][:, 0:P * SLOTS], start=True, stop=True)\
                    .then_inc(mixed, 1)

            def turn_z(g, turn, q, P):
                pe.wait_ge(z_ready, g + 1)
                wait(pe, z_copied, g - 1)
                for s in range(SLOTS):
                    last = nc.tensor.transpose(ps_zT[q % 2][:, s * P:(s + 1) * P], z[q][0:P, s, :], C["ident"][0:P, 0:P])
                last.then_inc(z_turned, 1)

            def turn_h(g, turn, q, P):
                pe.wait_ge(h_copied, g + 1)
                wait(pe, res_ready, g - 1)
                for s in range(SLOTS):
                    last = nc.tensor.transpose(ps_h[q % 2][0:P, s * D:(s + 1) * D], hT[q][:, s * P:(s + 1) * P],
                                               C["ident"][:, :])
                last.then_inc(h_turned, 1)
            sweep(pe, NODE_FULL, NODE_TAIL, (3, turn_h), (1, mix), (0, turn_z), unroll=DEEP)

        @block.scalar
        def _(act):
            def copy_h(g, turn, q, P):
                act.wait_ge(mixed, g + 1)
                act.wait_ge(stats_done, g + 1)
                wait(act, h_turned, g - DEEP + 1)
                nc.scalar.copy(hT[q][:, 0:P * SLOTS], ps_hT[q % 2][:, 0:P * SLOTS]).then_inc(h_copied, 1)

            def copy_z(g, turn, q, P):
                act.wait_ge(z_turned, g + 1)
                wait(act, mixed, g - DEEP + 1)
                nc.scalar.copy(zT[q][:, 0:P * SLOTS], ps_zT[q % 2][:, 0:P * SLOTS]).then_inc(z_copied, 1)

            def copy_rows(g, turn, q, P):
                act.wait_ge(h_turned, g + 1)
                if kind == 1:
                    act.wait_ge(dinv_ready, g + 1)
                wait(act, stored[q], DMA * turn)
                nc.scalar.copy(res[q][0:P, :, 0:D], ps_h[q % 2][0:P, :].rearrange("p (s c) -> p s c", c=D))\
                    .then_inc(res_ready, 1)
            sweep(act, NODE_FULL, NODE_TAIL, (3, copy_rows), (2, copy_h), (0, copy_z), unroll=DEEP)


def last_nodes(nc, C, x, table, sums, out):
    ph, DEEP = "n3", 6
    POOL_SLOTS = 3
    with ExitStack() as ctx:
        one = lambda name, shape, dt=F32: ctx.enter_context(nc.sbuf_tensor(f"{ph}_{name}", shape, dt))
        sb = lambda name, shape, dt=F32: [one(f"{name}{q}", shape, dt) for q in range(DEEP)]
        ps = lambda name, banks=1: [ctx.enter_context(nc.psum_tensor(f"{ph}_{name}{q}", [128, banks, GROUP], F32))
                                    for q in range(2)]
        sem = lambda name: ctx.enter_context(nc.semaphore(f"{ph}_{name}"))
        rows, sin, xin = (sb(n, [128, SLOTS, D]) for n in ("rows", "sin", "xin"))
        a, y, v, h, y2, res = (sb(n, [128, SLOTS, D]) for n in ("a", "y", "v", "h", "y2", "res"))
        both = sb("both", [128, 2, GROUP])
        st, st2 = sb("st", [128, SLOTS, 6]), sb("st2", [128, SLOTS, 6])
        mv, mv2 = sb("mv", [128, SLOTS, 2]), sb("mv2", [128, SLOTS, 2])
        sd, rstd, off, sd2, rstd2, off2 = (sb(n, [128, SLOTS]) for n in ("sd", "rstd", "off", "sd2", "rstd2", "off2"))
        ps_both, ps_out = ps("ps_both", 2), ps("ps_out")
        loaded = [sem(f"loaded{q}") for q in range(DEEP)]
        stored = [sem(f"stored{q}") for q in range(DEEP)]
        st_ready, st2_ready, inverse1, inverse2, a_ready, y_ready, y2_ready = (
            sem(n) for n in ("st_ready", "st2_ready", "inverse1", "inverse2", "a_ready", "y_ready", "y2_ready"))
        var, root, norm1, var2, root2, norm2 = (sem(n) for n in ("var", "root", "norm1", "var2", "root2", "norm2"))
        v_ready, turned, copied, mixed, h_ready, res_pool, res_act, a_scaled = (
            sem(n) for n in ("v_ready", "turned", "copied", "mixed", "h_ready", "res_pool", "res_act", "a_scaled"))
        block = ctx.enter_context(nc.Block())

        @block.sync
        def _(sp):
            def load(g, turn, q, P):
                wait(sp, y_ready, g - DEEP + 1)
                wait(sp, turned, g - DEEP + 1)
                sp.dma_start(rows[q][0:P], row_groups(table, g, P)).then_inc(loaded[q], DMA)
                sp.dma_start(sin[q][0:P], row_groups(sums, g, P)).then_inc(loaded[q], DMA)
                sp.dma_start(xin[q][0:P], row_groups(x, g, P)).then_inc(loaded[q], DMA)

            def store(g, turn, q, P):
                sp.wait_ge(res_pool, g + 1)
                sp.wait_ge(res_act, g + 1)
                sp.dma_start(row_groups(out, g, P), res[q][0:P]).then_inc(stored[q], DMA)
            sweep(sp, NODE_FULL, NODE_TAIL, (0, load), (11, store), unroll=DEEP)
            for q in range(DEEP):
                sp.wait_ge(stored[q], DMA * len(range(q, NODE_GROUPS, DEEP)))

        @block.gpsimd
        def _(pool):
            def scale(g, turn, q, P):
                pool.wait_ge(loaded[q], 3 * DMA * turn + 3 * DMA)
                wait(pool, y_ready, g - DEEP + 1)
                nc.gpsimd.tensor_tensor(a[q][0:P], rows[q][0:P], C["bn_rows2"][0:P, 0:1, :].to_broadcast([P, SLOTS, D]),
                                        ALU.mult).then_inc(a_scaled, 1)

            def shift(g, turn, q, P):
                pool.wait_ge(a_scaled, g + 1)
                nc.gpsimd.tensor_tensor(a[q][0:P], a[q][0:P], C["bn_rows2"][0:P, 1:2, :].to_broadcast([P, SLOTS, D]),
                                        ALU.add).then_inc(a_ready, 1)

            def norm_out(g, turn, q, P):
                wait_apart(pool, C, (norm2, g + 1), (stored[q], DMA * turn))
                for s in range(POOL_SLOTS):
                    last = nc.gpsimd.tensor_scalar(res[q][0:P, s, :], y2[q][0:P, s, :], rstd2[q][0:P, s:s + 1],
                                                   off2[q][0:P, s:s + 1], ALU.mult, ALU.add)
                last.then_inc(res_pool, 1)
            sweep(pool, NODE_FULL, NODE_TAIL, (0, scale), (9, norm_out), (0, shift), unroll=DEEP)

        @block.vector
        def _(dve):
            def to_y(g, turn, q, P):
                dve.wait_ge(a_ready, g + 1)
                dve.wait_ge(loaded[q], 3 * DMA * turn + 3 * DMA)
                wait(dve, v_ready, g - DEEP + 1)
                nc.vector.scalar_tensor_tensor(y[q][0:P], a[q][0:P], 0.0, xin[q][0:P], ALU.max, ALU.add)\
                    .then_inc(y_ready, 1)

            def to_y2(g, turn, q, P):
                dve.wait_ge(h_ready, g + 1)
                wait(dve, res_pool, g - DEEP + 1)
                wait(dve, res_act, g - DEEP + 1)
                nc.vector.scalar_tensor_tensor(y2[q][0:P], v[q][0:P], 2.0, h[q][0:P], ALU.mult, ALU.add)\
                    .then_inc(y2_ready, 1)

            def stats_of(rows, ready, parts, done):
                def stats(g, turn, q, P):
                    dve.wait_ge(ready, g + 1)
                    for s in range(SLOTS):
                        last = nc.vector.bn_stats(parts[q][0:P, s, :], rows[q][0:P, s, :])
                    last.then_inc(done, 1)
                return stats

            def variance_of(parts, ready, mean_var, done):
                def variance(g, turn, q, P):
                    wait_apart(dve, C, (ready, g + 1))
                    for s in range(SLOTS):
                        last = nc.vector.bn_aggr(mean_var[q][0:P, s, :], parts[q][0:P, s, :])
                    last.then_inc(done, 1)
                return variance

            def inverse_of(deviation, ready, inverse, done):
                def invert(g, turn, q, P):
                    dve.wait_ge(ready, g + 1)
                    nc.vector.reciprocal(inverse[q][0:P, :], deviation[q][0:P, :]).then_inc(done, 1)
                return invert

            def shift_of(mean_var, inverse, ready, shift, done):
                def negate(g, turn, q, P):
                    dve.wait_ge(ready, g + 1)
                    nc.vector.scalar_tensor_tensor(shift[q][0:P, :], mean_var[q][0:P, :, 0], -1.0, inverse[q][0:P, :],
                                                   ALU.mult, ALU.mult).then_inc(done, 1)
                return negate
            sweep(dve, NODE_FULL, NODE_TAIL, (0, to_y), (5, to_y2), (0, stats_of(y, y_ready, st, st_ready)),
                  (7, shift_of(mv2, rstd2, inverse2, off2, norm2)), (1, shift_of(mv, rstd, inverse1, off, norm1)),
                  (0, variance_of(st, st_ready, mv, var)), (5, stats_of(y2, y2_ready, st2, st2_ready)),
                  (6, inverse_of(sd2, root2, rstd2, inverse2)), (0, inverse_of(sd, root, rstd, inverse1)),
                  (5, variance_of(st2, st2_ready, mv2, var2)), unroll=DEEP)

        @block.tensor
        def _(pe):
            def turn_both(g, turn, q, P):
                pe.wait_ge(v_ready, g + 1)
                pe.wait_ge(loaded[q], 3 * DMA * turn + 3 * DMA)
                wait(pe, copied, g - 1)
                for s in range(SLOTS):
                    nc.tensor.transpose(ps_both[q % 2][:, 0, s * P:(s + 1) * P], v[q][0:P, s, :], C["ident"][0:P, 0:P])
                for s in range(SLOTS):
                    last = nc.tensor.transpose(ps_both[q % 2][:, 1, s * P:(s + 1) * P], sin[q][0:P, s, :], C["ident"][0:P, 0:P])
                last.then_inc(turned, 1)

            def mix(g, turn, q, P):
                pe.wait_ge(copied, g + 1)
                wait(pe, h_ready, g - 1)
                nc.tensor.matmul(ps_out[q % 2][0:P, 0, :], C["ones3"][:, 0:P], C["bc_parts"][:, :], start=True, stop=False)
                for s in range(SLOTS):
                    o = ps_out[q % 2][0:P, 0, s * D:(s + 1) * D]
                    nc.tensor.matmul(o, both[q][:, 0, s * P:(s + 1) * P], C["Wc_x"][:, :], start=False, stop=False)
                    last = nc.tensor.matmul(o, both[q][:, 1, s * P:(s + 1) * P], C["Wc_a"][:, :], start=False,
                                            stop=s == SLOTS - 1)
                last.then_inc(mixed, 1)
            sweep(pe, NODE_FULL, NODE_TAIL, (2, mix), (0, turn_both), unroll=DEEP)

        @block.scalar
        def _(act):
            def relu(g, turn, q, P):
                act.wait_ge(mixed, g + 1)
                wait(act, y2_ready, g - DEEP + 1)
                nc.scalar.activation(h[q][0:P].rearrange("p s c -> p (s c)"), ps_out[q % 2][0:P, 0, :], ACT.Relu)\
                    .then_inc(h_ready, 1)

            def root1(g, turn, q, P):
                act.wait_ge(var, g + 1)
                nc.scalar.activation(sd[q][0:P, :], mv[q][0:P, :, 1], ACT.Sqrt, bias=C["eps"][0:P, :]).then_inc(root, 1)

            def root_2(g, turn, q, P):
                act.wait_ge(var2, g + 1)
                nc.scalar.activation(sd2[q][0:P, :], mv2[q][0:P, :, 1], ACT.Sqrt, bias=C["eps"][0:P, :]).then_inc(root2, 1)

            def norm_v(g, turn, q, P):
                act.wait_ge(norm1, g + 1)
                wait(act, turned, g - DEEP + 1)
                wait(act, y2_ready, g - DEEP + 1)
                for s in range(SLOTS):
                    last = nc.scalar.activation(v[q][0:P, s, :], y[q][0:P, s, :], ACT.Identity,
                                                bias=off[q][0:P, s:s + 1], scale=rstd[q][0:P, s:s + 1])
                last.then_inc(v_ready, 1)

            def copy(g, turn, q, P):
                act.wait_ge(turned, g + 1)
                wait(act, mixed, g - DEEP + 1)
                nc.scalar.copy(both[q][:, :, 0:P * SLOTS], ps_both[q % 2][:, :, 0:P * SLOTS]).then_inc(copied, 1)

            def norm_rest(g, turn, q, P):
                act.wait_ge(norm2, g + 1)
                wait(act, stored[q], DMA * turn)
                for s in range(POOL_SLOTS, SLOTS):
                    last = nc.scalar.activation(res[q][0:P, s, :], y2[q][0:P, s, :], ACT.Identity,
                                                bias=off2[q][0:P, s:s + 1], scale=rstd2[q][0:P, s:s + 1])
                last.then_inc(res_act, 1)
            sweep(act, NODE_FULL, NODE_TAIL, (5, relu), (2, norm_v), (3, copy), (6, root_2), (9, norm_rest),
                  (0, root1), unroll=DEEP)


def norm_rows(nc, C, ph, first, bn_rows):
    with ExitStack() as ctx:
        one = lambda name, shape: ctx.enter_context(nc.sbuf_tensor(f"{ph}_{name}", shape, F32))
        mv = one("mv", [D, 2])
        sd = one("sd", [D, 1])
        ss = one("ss", [D, 2])
        mb = one("mb", [D, 1])
        wide = one("wide", [D, 2, 128])
        pr = ctx.enter_context(nc.psum_tensor(f"{ph}_ps", [128, 2 * D], F32))
        sem = lambda name: ctx.enter_context(nc.semaphore(f"{ph}_{name}"))
        chain_sem, var_ready, sd_ready, wide_ready, rows_ready = (sem(n) for n in ("chain", "var", "sd", "wide", "rows"))
        block = ctx.enter_context(nc.Block())
        b, gamma, beta = (C["vectors"][:, first + i:first + i + 1] for i in range(3))

        @block.vector
        def _(dve):
            ch = Chain(dve, chain_sem)
            ch.start(0)
            nc.vector.bn_aggr(mv[:, :], C["stats"][:, :]).then_inc(var_ready, 1)
            dve.wait_ge(sd_ready, 1)
            ch.link(nc.vector.reciprocal(sd[:, :], sd[:, :]))
            ch.link(nc.vector.tensor_tensor(mb[:, :], mv[:, 0:1], b, ALU.add))
            ch.link(nc.vector.tensor_tensor(ss[:, 0:1], gamma, sd[:, :], ALU.mult))
            ch.link(nc.vector.tensor_tensor(mb[:, :], b, mb[:, :], ALU.subtract))
            ch.link(nc.vector.tensor_tensor(mb[:, :], mb[:, :], ss[:, 0:1], ALU.mult))
            ch.link(nc.vector.tensor_tensor(ss[:, 1:2], mb[:, :], beta, ALU.add))
            nc.vector.tensor_copy(wide[:, :, :], ss[:, :].unsqueeze(2).to_broadcast([D, 2, 128])).then_inc(wide_ready, 1)
            dve.wait_ge(rows_ready, 1)
            nc.vector.tensor_copy(bn_rows[:, :, :], pr[:, :].rearrange("p (a c) -> p a c", a=2))

        @block.scalar
        def _(act):
            act.wait_ge(var_ready, 1)
            nc.scalar.activation(sd[:, :], mv[:, 1:2], ACT.Sqrt, bias=C["eps"][:, :]).then_inc(sd_ready, 1)

        @block.tensor
        def _(pe):
            pe.wait_ge(wide_ready, 1)
            for i in range(2):
                last = nc.tensor.matmul(pr[:, i * D:(i + 1) * D], wide[:, i, :], C["ident"][:, :], start=True, stop=True)
            last.then_inc(rows_ready, 1)


_INS = ["x", "src", "dst", "edge_weight", "L0_gnn_W1", "L0_gnn_b1", "L0_gnn_W2", "L0_gnn_b2", "L0_gnn_g1",
        "L0_gnn_beta1", "L0_gnn_g2", "L0_gnn_beta2", "L1_gnn_factors", "L1_gnn_Wm", "L1_gnn_bm", "L1_gnn_Wc",
        "L1_gnn_bc"]


def kernel(**inputs):
    import numpy as _np
    import concourse.bacc as _bacc
    from concourse import mybir as _mybir
    from concourse.bass_utils import run_bass_kernel_spmd as _run

    nc = _bacc.Bacc("TRN2", target_bir_lowering=False, num_devices=1)
    arrays, args = {}, []
    for name in _INS:
        a = _np.ascontiguousarray(inputs[name])
        arrays[f"in_{name}"] = a
        args.append(nc.dram_tensor(f"in_{name}", a.shape, _mybir.dt.from_np(a.dtype), kind="ExternalInput").ap())
    out = nc.dram_tensor("out_0", (N, D), F32, kind="ExternalOutput").ap()
    build(nc, *args, out)
    r = _run(nc, [arrays], core_ids=[0])
    return r.results[0]["out_0"]
```
